# Optimizing a Trainium2 kernel written in Bass

```python
import numpy as np
import jax
import jax.numpy as jnp

def _softmax(x, axis=-1):
    return jax.nn.softmax(x, axis=axis)

def _gelu(x):
    return jax.nn.gelu(x, approximate=True)

def _silu(x):
    return jax.nn.silu(x)

def _sigmoid(x):
    return jax.nn.sigmoid(x)

def _layernorm(x, axis=-1, eps=1e-05):
    m = jnp.mean(x, axis=axis, keepdims=True)
    v = jnp.var(x, axis=axis, keepdims=True)
    return (x - m) / jnp.sqrt(v + eps)

def _scatter_add(tgt, idx, src, axis=0):
    return tgt.at[idx].add(src)

def _segment_sum(src, seg, n):
    return jax.ops.segment_sum(src, seg, n)
kernel_name = 'mk_gnn_preln_d4_gnn_r32_a4ff93'

def setup_inputs(seed: int=0):
    np.random.seed(seed)
    _w = jnp.asarray

    def _rec_inputs():
        import jax
        import jax.numpy as jnp
        _gk = jax.random.key(seed)
        x = -0.000202 + 1 * jax.random.normal(jax.random.fold_in(_gk, 1), (50000, 128), jnp.float32)
        src = jax.random.randint(jax.random.fold_in(_gk, 2), (25000,), 0, 50000, jnp.int32)
        dst = jnp.minimum((50000 * jax.random.uniform(jax.random.fold_in(_gk, 3), (25000,)) ** 2.0).astype(jnp.int32), 49999)
        _o = jnp.argsort(dst, stable=True)
        src = src[_o]
        dst = dst[_o]
        return (x, src, dst)
    x, src, dst = _rec_inputs()

    def _L0_gnn_setup():
        import jax, jax.numpy as jnp
        import numpy as np
        N = 50000
        E = 25000
        G_DIM = 128
        HEADS = 8
        DEPTH = 3
        EPS = 1e-05

        def _ln(x, w, b):
            m = jnp.mean(x, axis=-1, keepdims=True)
            v = jnp.var(x, axis=-1, keepdims=True)
            return (x - m) * jax.lax.rsqrt(v + EPS) * w + b

        def _graph_attention(x, src, dst, nin_w, nin_b, Wqkv):
            s = _ln(x, nin_w, nin_b)
            qkv = s @ Wqkv
            q, k, v = jnp.split(qkv, 3, axis=-1)
            D = G_DIM // HEADS
            q = q.reshape(N, HEADS, D)
            k = k.reshape(N, HEADS, D)
            v = v.reshape(N, HEADS, D)
            scale = G_DIM ** (-0.5)
            att = q[src] * k[dst] * scale
            mx = jax.ops.segment_max(att, dst, num_segments=N)
            e = jnp.exp(att - mx[dst])
            z = jax.ops.segment_sum(e, dst, num_segments=N)
            a = e / z[dst]
            rst = jax.ops.segment_sum(v[src] * a, dst, num_segments=N)
            return rst.reshape(N, G_DIM)
        key = jax.random.key(seed)
        ks = jax.random.split(key, 12)
        s = 0.02
        inp = {'h': jax.random.normal(ks[0], (N, G_DIM), jnp.float32), 'src': jax.random.randint(ks[1], (E,), 0, N, jnp.int32), 'dst': jax.random.randint(ks[2], (E,), 0, N, jnp.int32), 'norm_w': jnp.ones((G_DIM,), jnp.float32), 'norm_b': jnp.zeros((G_DIM,), jnp.float32), 'nin_w': jnp.ones((G_DIM,), jnp.float32), 'nin_b': jnp.zeros((G_DIM,), jnp.float32), 'Wqkv': jax.random.normal(ks[3], (G_DIM, 3 * G_DIM), jnp.float32) * s, 'no_w': jnp.ones((G_DIM,), jnp.float32), 'no_b': jnp.zeros((G_DIM,), jnp.float32), 'W1': jax.random.normal(ks[4], (G_DIM, 4 * G_DIM), jnp.float32) * s, 'b1': jnp.zeros((4 * G_DIM,), jnp.float32), 'W2': jax.random.normal(ks[5], (4 * G_DIM, G_DIM), jnp.float32) * s, 'b2': jnp.zeros((G_DIM,), jnp.float32)}
        return inp
    _L0_gnn_all = _L0_gnn_setup()
    _L0_gnn_in = {k: v for k, v in _L0_gnn_all.items() if k in ('norm_w', 'norm_b', 'nin_w', 'nin_b', 'Wqkv', 'no_w', 'no_b', 'W1', 'b1', 'W2', 'b2')}
    del _L0_gnn_all

    def _L1_gnn_setup():
        import jax, jax.numpy as jnp
        import numpy as np
        N = 50000
        E = 50000
        IN_DIM = 128
        HEADS = 4
        OUT_DIM = 32
        NEG_SLOPE = 0.2
        key = jax.random.key(seed)
        k1, k2, k3, k4, k5, k6 = jax.random.split(key, 6)
        x = jax.random.normal(k1, (N, IN_DIM), dtype=jnp.float32)
        src = jax.random.randint(k2, (E,), 0, N)
        dst = jax.random.randint(k3, (E,), 0, N)
        edge_index = jnp.stack([src, dst], axis=0).astype(jnp.int64)
        W = jax.random.normal(k4, (IN_DIM, HEADS * OUT_DIM), dtype=jnp.float32) * 0.08
        att = jax.random.normal(k5, (HEADS, 2 * OUT_DIM), dtype=jnp.float32) * 0.1
        bias = jnp.zeros((HEADS * OUT_DIM,), dtype=jnp.float32)
        return {'x': x, 'edge_index': edge_index, 'W': W, 'att': att, 'bias': bias}
    _L1_gnn_all = _L1_gnn_setup()
    _L1_gnn_in = {k: v for k, v in _L1_gnn_all.items() if k in ('W', 'att', 'bias')}
    del _L1_gnn_all

    def _L2_gnn_setup():
        import jax, jax.numpy as jnp
        import numpy as np
        N_NODES = 1250
        key = jax.random.key(seed)
        k1, k2, k3, k4 = jax.random.split(key, 4)
        ndata = jax.random.normal(k1, (N_NODES, 128), dtype=jnp.float32)
        src = jax.random.randint(k2, (20000,), 0, N_NODES, dtype=jnp.int32)
        dst = jax.random.randint(k3, (20000,), 0, N_NODES, dtype=jnp.int32)
        W = jax.random.normal(k4, (128, 128), dtype=jnp.float32) / np.sqrt(128.0)
        b = jnp.zeros((128,), dtype=jnp.float32)
        return {'ndata': ndata, 'src': src, 'dst': dst, 'W': W, 'b': b}
    _L2_gnn_all = _L2_gnn_setup()
    _L2_gnn_in = {k: v for k, v in _L2_gnn_all.items() if k in ('W', 'b')}
    del _L2_gnn_all

    def _L3_gnn_setup():
        import jax, jax.numpy as jnp
        import numpy as np
        N_NODES = 3125
        N_EDGES = 50000
        D_IN = 128
        D_HID = 128
        D_OUT = 128
        key = jax.random.key(seed)
        ks = jax.random.split(key, 10)
        s = 0.05
        return {'x': jax.random.normal(ks[0], (N_NODES, D_IN), jnp.float32), 'src': jax.random.randint(ks[1], (N_EDGES,), 0, N_NODES, jnp.int32), 'dst': jax.random.randint(ks[2], (N_EDGES,), 0, N_NODES, jnp.int32), 'W_neigh': jax.random.normal(ks[3], (D_IN, D_HID), jnp.float32) * s, 'W_self': jax.random.normal(ks[4], (D_IN, D_HID), jnp.float32) * s, 'b_self': jax.random.normal(ks[5], (D_HID,), jnp.float32) * s, 'W_fc1': jax.random.normal(ks[6], (D_HID, D_HID), jnp.float32) * s, 'b_fc1': jax.random.normal(ks[7], (D_HID,), jnp.float32) * s, 'W_fc2': jax.random.normal(ks[8], (D_HID, D_OUT), jnp.float32) * s, 'b_fc2': jax.random.normal(ks[9], (D_OUT,), jnp.float32) * s}
    _L3_gnn_all = _L3_gnn_setup()
    _L3_gnn_in = {k: v for k, v in _L3_gnn_all.items() if k in ('W_neigh', 'W_self', 'b_self', 'W_fc1', 'b_fc1', 'W_fc2', 'b_fc2')}
    del _L3_gnn_all
    return {'x': x, 'src': src, 'dst': dst, 'L0_gnn_norm_w': _L0_gnn_in['norm_w'], 'L0_gnn_norm_b': _L0_gnn_in['norm_b'], 'L0_gnn_nin_w': _L0_gnn_in['nin_w'], 'L0_gnn_nin_b': _L0_gnn_in['nin_b'], 'L0_gnn_Wqkv': _L0_gnn_in['Wqkv'], 'L0_gnn_no_w': _L0_gnn_in['no_w'], 'L0_gnn_no_b': _L0_gnn_in['no_b'], 'L0_gnn_W1': _L0_gnn_in['W1'], 'L0_gnn_b1': _L0_gnn_in['b1'], 'L0_gnn_W2': _L0_gnn_in['W2'], 'L0_gnn_b2': _L0_gnn_in['b2'], 'L1_gnn_W': _L1_gnn_in['W'], 'L1_gnn_att': _L1_gnn_in['att'], 'L1_gnn_bias': _L1_gnn_in['bias'], 'L2_gnn_W': _L2_gnn_in['W'], 'L2_gnn_b': _L2_gnn_in['b'], 'L3_gnn_W_neigh': _L3_gnn_in['W_neigh'], 'L3_gnn_W_self': _L3_gnn_in['W_self'], 'L3_gnn_b_self': _L3_gnn_in['b_self'], 'L3_gnn_W_fc1': _L3_gnn_in['W_fc1'], 'L3_gnn_b_fc1': _L3_gnn_in['b_fc1'], 'L3_gnn_W_fc2': _L3_gnn_in['W_fc2'], 'L3_gnn_b_fc2': _L3_gnn_in['b_fc2']}

def reference(x, src, dst, L0_gnn_norm_w, L0_gnn_norm_b, L0_gnn_nin_w, L0_gnn_nin_b, L0_gnn_Wqkv, L0_gnn_no_w, L0_gnn_no_b, L0_gnn_W1, L0_gnn_b1, L0_gnn_W2, L0_gnn_b2, L1_gnn_W, L1_gnn_att, L1_gnn_bias, L2_gnn_W, L2_gnn_b, L3_gnn_W_neigh, L3_gnn_W_self, L3_gnn_b_self, L3_gnn_W_fc1, L3_gnn_b_fc1, L3_gnn_W_fc2, L3_gnn_b_fc2):
    import jax
    import jax.numpy as jnp

    def _L0_gnn_ref(h, src, dst, norm_w, norm_b, nin_w, nin_b, Wqkv, no_w, no_b, W1, b1, W2, b2):
        import jax, jax.numpy as jnp
        import numpy as np
        N = 50000
        E = 25000
        G_DIM = 128
        HEADS = 8
        DEPTH = 3
        EPS = 1e-05

        def _ln(x, w, b):
            m = jnp.mean(x, axis=-1, keepdims=True)
            v = jnp.var(x, axis=-1, keepdims=True)
            return (x - m) * jax.lax.rsqrt(v + EPS) * w + b

        def _graph_attention(x, src, dst, nin_w, nin_b, Wqkv):
            s = _ln(x, nin_w, nin_b)
            qkv = s @ Wqkv
            q, k, v = jnp.split(qkv, 3, axis=-1)
            D = G_DIM // HEADS
            q = q.reshape(N, HEADS, D)
            k = k.reshape(N, HEADS, D)
            v = v.reshape(N, HEADS, D)
            scale = G_DIM ** (-0.5)
            att = q[src] * k[dst] * scale
            mx = jax.ops.segment_max(att, dst, num_segments=N)
            e = jnp.exp(att - mx[dst])
            z = jax.ops.segment_sum(e, dst, num_segments=N)
            a = e / z[dst]
            rst = jax.ops.segment_sum(v[src] * a, dst, num_segments=N)
            return rst.reshape(N, G_DIM)
        for _ in range(DEPTH):
            x = _ln(h, norm_w, norm_b)
            x = _graph_attention(x, src, dst, nin_w, nin_b, Wqkv)
            y = _ln(x, no_w, no_b)
            y = jax.nn.gelu(y @ W1 + b1, approximate=False) @ W2 + b2
            h = y + h
        return h

    def _L1_gnn_ref(x, edge_index, W, att, bias):
        import jax, jax.numpy as jnp
        import numpy as np
        N = 50000
        E = 50000
        IN_DIM = 128
        HEADS = 4
        OUT_DIM = 32
        NEG_SLOPE = 0.2
        src, dst = (edge_index[0], edge_index[1])
        n = x.shape[0]
        Wh = (x @ W).reshape(n, HEADS, OUT_DIM)
        a_src = jnp.einsum('nhf,hf->nh', Wh, att[:, :OUT_DIM])
        a_dst = jnp.einsum('nhf,hf->nh', Wh, att[:, OUT_DIM:])
        logits = jax.nn.leaky_relu(a_src[src] + a_dst[dst], negative_slope=NEG_SLOPE)
        seg_max = jax.ops.segment_max(logits, dst, num_segments=n)
        exp_s = jnp.exp(logits - seg_max[dst])
        denom = jnp.clip(jax.ops.segment_sum(exp_s, dst, num_segments=n), 1e-09, None)
        alpha = exp_s / denom[dst]
        messages = alpha[:, :, None] * Wh[src]
        out = jax.ops.segment_sum(messages.reshape(-1, HEADS * OUT_DIM), dst, num_segments=n)
        return out + bias

    def _L2_gnn_ref(ndata, src, dst, W, b):
        import jax, jax.numpy as jnp
        import numpy as np
        N_NODES = 1250
        n = ndata.shape[0]
        agg = jax.ops.segment_sum(ndata[src], dst, num_segments=n)
        deg = jax.ops.segment_sum(jnp.ones_like(src, dtype=ndata.dtype), dst, num_segments=n)
        mean = agg / jnp.maximum(deg, 1.0)[:, None]
        h = ndata + mean
        return h @ W.T + b

    def _L3_gnn_ref(x, src, dst, W_neigh, W_self, b_self, W_fc1, b_fc1, W_fc2, b_fc2):
        import jax, jax.numpy as jnp
        import numpy as np
        N_NODES = 3125
        N_EDGES = 50000
        D_IN = 128
        D_HID = 128
        D_OUT = 128
        n = x.shape[0]
        msg = x[src]
        agg = jax.ops.segment_sum(msg, dst, num_segments=n)
        deg = jax.ops.segment_sum(jnp.ones((src.shape[0],), x.dtype), dst, num_segments=n)
        h_neigh = agg / jnp.maximum(deg, 1.0)[:, None]
        h = x @ W_self + b_self + h_neigh @ W_neigh
        h = jax.nn.relu(h)
        h = jax.nn.relu(h @ W_fc1 + b_fc1)
        return h @ W_fc2 + b_fc2
    edge_index = jnp.stack([src, dst])
    h = jnp.maximum(_layernorm(x, axis=-1), 0.0)
    x = x + _L0_gnn_ref(h, src, dst, L0_gnn_norm_w, L0_gnn_norm_b, L0_gnn_nin_w, L0_gnn_nin_b, L0_gnn_Wqkv, L0_gnn_no_w, L0_gnn_no_b, L0_gnn_W1, L0_gnn_b1, L0_gnn_W2, L0_gnn_b2)
    h = jnp.maximum(_layernorm(x, axis=-1), 0.0)
    x = x + _L1_gnn_ref(h, edge_index, L1_gnn_W, L1_gnn_att, L1_gnn_bias)
    h = jnp.maximum(_layernorm(x, axis=-1), 0.0)
    x = x + _L2_gnn_ref(h, src, dst, L2_gnn_W, L2_gnn_b)
    h = jnp.maximum(_layernorm(x, axis=-1), 0.0)
    x = x + _L3_gnn_ref(h, src, dst, L3_gnn_W_neigh, L3_gnn_W_self, L3_gnn_b_self, L3_gnn_W_fc1, L3_gnn_b_fc1, L3_gnn_W_fc2, L3_gnn_b_fc2)
    return x

_drawn_inputs = setup_inputs


def setup_inputs(seed=0):
    import zlib

    import numpy as np

    out = dict(_drawn_inputs(seed))
    spreads = {'L0_gnn_norm_w': (1.0, 0.6),
     'L0_gnn_norm_b': (0.0, 0.8),
     'L0_gnn_nin_w': (1.0, 0.6),
     'L0_gnn_nin_b': (0.0, 0.8),
     'L0_gnn_no_w': (1.0, 0.6),
     'L0_gnn_no_b': (0.0, 0.8),
     'L0_gnn_b1': (0.0, 0.1),
     'L0_gnn_b2': (0.0, 0.1),
     'L1_gnn_bias': (0.0, 0.1),
     'L2_gnn_b': (0.0, 0.1)}
    factors = {'L1_gnn_att': 4.961, 'L3_gnn_W_neigh': 3.444, 'L3_gnn_b_self': 8.0, 'L3_gnn_b_fc1': 5.947}
    for name, (base, spread) in spreads.items():
        noise = np.random.default_rng([zlib.crc32(name.encode()), seed]).standard_normal(out[name].shape)
        drawn = base * np.exp(spread * noise) if base else spread * noise
        out[name] = jnp.asarray(drawn.astype(out[name].dtype))
    for name, factor in factors.items():
        out[name] = (out[name] * factor).astype(out[name].dtype)
    return out
```

```python
from contextlib import ExitStack

import concourse.bass as bass
from concourse import mybir

F32 = mybir.dt.float32
I32 = mybir.dt.int32
BF16 = mybir.dt.bfloat16
ALU = mybir.AluOpType
ACT = mybir.ActivationFunctionType
AX = bass.IndirectOffsetOnAxis

P = 128
D = 128
N = 50000
E = 25000
TILES = 4
CHUNK = TILES * P
EDGE_CHUNKS = 50
NODE_CHUNKS = 98
NP = NODE_CHUNKS * CHUNK
EP = EDGE_CHUNKS * CHUNK
HIDDEN = 4 * D
HC = HIDDEN // P
ROUNDS = 3
HEADS = 4
HEAD = D // HEADS
EPS = 1e-5
GAP = -(2.0 ** 100)
SKIP = 1 << 20
QK_SCALE = float(D) ** -0.5
RING = 8
DMA = 16


def run_slots(eng, n, first, stages):
    deepest = max(lag for lag, _ in stages)
    assert deepest <= first and (n - first) % 2 == 0

    def slot(s):
        for lag, body in stages:
            if 0 <= s - lag < n:
                body(s - lag, (s - lag) % 2)

    for s in range(first):
        slot(s)
    with eng.Fori(0, (n - first) // 2) as i:
        twice = eng.snap(2 * i)
        for k in range(2):
            for lag, body in stages:
                body(twice + (first + k - lag), (first + k - lag) % 2)
    for s in range(n, n + deepest):
        slot(s)


def later(c, n):
    return not isinstance(c, int) or c >= n


def tile(ap, j, width=D):
    return ap[:, j * width:(j + 1) * width]


def alloc(nc, ctx, made, names, shape, dt=F32, space="sbuf"):
    make = nc.sbuf_tensor if space == "sbuf" else nc.psum_tensor
    for name in names.split():
        made[name] = ctx.enter_context(make(f"{made['phase']}_{name}", shape, dt))


def semaphores(nc, ctx, made, names):
    for name in names.split():
        made[name] = ctx.enter_context(nc.semaphore(f"{made['phase']}_{name}"))


def wait_apart(eng, sem, value):
    if not isinstance(value, int):
        eng.wait_ge(sem, 1)
    eng.wait_ge(sem, value)


def row_stats(v, rows, stats, moments):
    for j, r in enumerate(rows):
        v.bn_stats(stats[:, 6 * j:6 * j + 6], r)
    v.drain()
    for j in range(len(rows)):
        last = v.bn_aggr(moments[:, 2 * j:2 * j + 2], stats[:, 6 * j:6 * j + 6])
    return last


def inverse_std(a, moments, log_var, rstd, n, eps_col):
    var = moments[:, 0:2 * n].rearrange("p (n two) -> p n two", two=2)[:, :, 1]
    a.activation(log_var[:, 0:n], var, ACT.Ln, bias=eps_col)
    a.drain()
    return a.activation(rstd[:, 0:n], log_var[:, 0:n], ACT.Exp, scale=-0.5)


def shift_of(v, shift, moments, rstd, n):
    mean = moments[:, 0:2 * n].rearrange("p (n two) -> p n two", two=2)[:, :, 0]
    return v.scalar_tensor_tensor(shift[:, 0:n], mean, -1.0, rstd[:, 0:n], ALU.mult, ALU.mult)


def scale_and_shift(a, outs, rows, rstd, shift):
    for j, (o, r) in enumerate(zip(outs, rows)):
        last = a.activation(o, r, ACT.Identity, bias=shift[:, j:j + 1], scale=rstd[:, j:j + 1])
    return last


def log_exp_tables(a):
    return lambda c, k: a.preload_act_table_set("natural_log_exp_and_others") if k == 0 else None


def normalise(v, outs, rows, moments, rstd, at=0):
    for j, (o, r) in enumerate(zip(outs, rows)):
        k = at + j
        last = v.tensor_scalar(o, r, moments[:, 2 * k:2 * k + 1], rstd[:, k:k + 1],
                               ALU.subtract, ALU.mult)
    return last


def setup(nc, w, inp):
    with ExitStack() as ctx:
        t = {"phase": "setup"}
        alloc(nc, ctx, t, "wqkv_raw", [P, 3 * D])
        alloc(nc, ctx, t, "w1_raw", [P, HIDDEN])
        alloc(nc, ctx, t, "nin_w nin_b no_w no_b asrc adst", [P, 1])
        alloc(nc, ctx, t, "b1_raw gelu_b1", [P, HC])
        alloc(nc, ctx, t, "w2l2_raw l1_wT block_src block_dst", [P, D])
        alloc(nc, ctx, t, "b2_row c0_row l1b_row", [1, D])
        alloc(nc, ctx, t, "c_row4", [1, CHUNK])
        alloc(nc, ctx, t, "dst_next", [P, EDGE_CHUNKS * TILES], I32)
        alloc(nc, ctx, t, "not_last", [P, EDGE_CHUNKS * TILES])
        alloc(nc, ctx, t, "cur0 cur1 prev0 prev1", [P, CHUNK], I32)
        alloc(nc, ctx, t, "same", [P, CHUNK])
        alloc(nc, ctx, t, "count0 count1", [P, CHUNK])
        alloc(nc, ctx, t, "ps_row", [1, CHUNK], F32, "psum")
        alloc(nc, ctx, t, "ps_a ps_b ps_c ps_d ps_cnt0 ps_cnt1", [P, CHUNK], F32, "psum")
        semaphores(nc, ctx, t,
                   "loaded dst_sem0 dst_sem1 zeroed ident_ready blocks pe_out dve_out act_out "
                   "counted count_cols count_used")
        cur, prev = (t["cur0"], t["cur1"]), (t["prev0"], t["prev1"])
        count, ps_cnt, dst_sem = (t["count0"], t["count1"]), (t["ps_cnt0"], t["ps_cnt1"]), (t["dst_sem0"], t["dst_sem1"])
        col = lambda x: x.rearrange("(p a) -> p a", a=1)
        row = lambda x: x.rearrange("(a n) -> a n", a=1)
        loads = [
            (t["wqkv_raw"][:, :], inp["L0_gnn_Wqkv"][:, :]),
            (t["w1_raw"][:, :], inp["L0_gnn_W1"][:, :]),
            (w["w2"][:, :].rearrange("p (j n) -> p j n", j=HC),
             inp["L0_gnn_W2"].rearrange("(j p) n -> p j n", p=P)),
            (t["nin_w"][:, :], col(inp["L0_gnn_nin_w"])), (t["nin_b"][:, :], col(inp["L0_gnn_nin_b"])),
            (t["no_w"][:, :], col(inp["L0_gnn_no_w"])), (t["no_b"][:, :], col(inp["L0_gnn_no_b"])),
            (t["b2_row"][:, :], row(inp["L0_gnn_b2"])),
            (w["norm_w"][:, :], inp["L0_gnn_norm_w"].partition_broadcast(P)),
            (w["norm_b"][:, :], inp["L0_gnn_norm_b"].partition_broadcast(P)),
            (w["l1_w"][:, :], inp["L1_gnn_W"][:, :]),
            (t["l1b_row"][:, :], row(inp["L1_gnn_bias"])),
            (t["w2l2_raw"][:, :], inp["L2_gnn_W"][:, :]),
            (w["l3_neigh"][:, :], inp["L3_gnn_W_neigh"][:, :]),
            (w["l3_self"][:, :], inp["L3_gnn_W_self"][:, :]),
            (w["l3_fc1"][:, :], inp["L3_gnn_W_fc1"][:, :]),
            (w["l3_fc2"][:, :], inp["L3_gnn_W_fc2"][:, :]),
            (w["l3_bself"][:, :], col(inp["L3_gnn_b_self"])),
            (w["l3_bfc1"][:, :], col(inp["L3_gnn_b_fc1"])),
            (w["src_idx"][:, :], inp["src_t"][:, :]), (w["dst_idx"][:, :], inp["dst_t"][:, :]),
            (t["dst_next"][:, :], inp["dst_next_t"][:, :]),
        ]
        for j in range(HC):
            loads.append((t["b1_raw"][:, j:j + 1], col(inp["L0_gnn_b1"][j * P:(j + 1) * P])))
        for h in range(HEADS):
            loads.append((t["asrc"][h * HEAD:(h + 1) * HEAD, :], col(inp["L1_gnn_att"][h, 0:HEAD])))
            loads.append((t["adst"][h * HEAD:(h + 1) * HEAD, :], col(inp["L1_gnn_att"][h, HEAD:2 * HEAD])))
        for j in range(TILES):
            loads.append((tile(w["l2_b4"], j), row(inp["L2_gnn_b"])))
            loads.append((tile(w["l3_b4"], j), row(inp["L3_gnn_b_fc2"])))
        block = ctx.enter_context(nc.Block())

        @block.sync
        def _(sp):
            for to, frm in loads:
                sp.dma_start(to, frm).then_inc(t["loaded"], DMA)
            for k in range(2):
                sp.dma_start(cur[k][:, :], inp["dst_ext"][1 + k * CHUNK:1 + (k + 1) * CHUNK].partition_broadcast(P))\
                  .then_inc(dst_sem[k], DMA)
                sp.dma_start(prev[k][:, :], inp["dst_ext"][k * CHUNK:(k + 1) * CHUNK].partition_broadcast(P))\
                  .then_inc(dst_sem[k], DMA)
            with sp.Fori(0, EDGE_CHUNKS // 2 - 1) as i:
                at = sp.snap(i * (2 * CHUNK))
                done = sp.snap(2 * i)
                for k in range(2):
                    wait_apart(sp, t["counted"], done + (k + 1))
                    sp.dma_start(cur[k][:, :], inp["dst_ext"][bass.ds(at + (1 + (2 + k) * CHUNK), CHUNK)].partition_broadcast(P))\
                      .then_inc(dst_sem[k], DMA)
                    sp.dma_start(prev[k][:, :], inp["dst_ext"][bass.ds(at + ((2 + k) * CHUNK), CHUNK)].partition_broadcast(P))\
                      .then_inc(dst_sem[k], DMA)

        @block.gpsimd
        def _(pool):
            pool.memset(w["ident"][:, :], 0.0).then_inc(t["zeroed"], 1)
            pool.memset(w["ones_row"][:, :], 1.0)
            pool.memset(w["eps_col"][:, :], EPS)
            pool.wait_ge(t["zeroed"], 1)
            pool.affine_select(out=w["ident"][:, :], in_=w["ident"][:, :], compare_op=ALU.not_equal, fill=1.0,
                               base=0, pattern=[[-1, P]], channel_multiplier=1).then_inc(t["ident_ready"], 1)

        @block.vector
        def _(v):
            v.memset(t["block_src"][:, :], 0.0)
            v.memset(t["block_dst"][:, :], 0.0)
            v.drain()
            for h in range(HEADS):
                for m in (t["block_src"], t["block_dst"]):
                    v.memset(m[h * HEAD:(h + 1) * HEAD, h * HEAD:(h + 1) * HEAD], 1.0)
            v.wait_ge(t["loaded"], DMA * len(loads))
            v.tensor_scalar(w["wqkv"][:, :], t["wqkv_raw"][:, :], t["nin_w"][:, 0:1], None, ALU.mult)
            v.tensor_scalar(w["w1"][:, :], t["w1_raw"][:, :], t["no_w"][:, 0:1], None, ALU.mult)
            v.drain()
            v.tensor_scalar(t["block_src"][:, :], t["block_src"][:, :], t["asrc"][:, 0:1], None, ALU.mult)
            v.tensor_scalar(t["block_dst"][:, :], t["block_dst"][:, :], t["adst"][:, 0:1], None, ALU.mult)\
             .then_inc(t["blocks"], 1)
            v.tensor_tensor(t["not_last"][:, :], w["dst_idx"][:, :], t["dst_next"][:, :], ALU.is_equal)
            v.drain()
            v.scalar_tensor_tensor(w["end_idx"][:, :], t["not_last"][:, :], float(SKIP), w["dst_idx"][:, :],
                                   ALU.mult, ALU.add)
            v.memset(w["lc4"][:, :], 0.0)
            v.wait_ge(t["pe_out"], 1)
            v.tensor_copy(w["bqkv"][:, :], t["ps_a"][:, 0:3])
            v.tensor_tensor(w["b1"][:, :], t["ps_a"][:, 4:4 + HC], t["b1_raw"][:, :], ALU.add)
            v.tensor_copy(w["l2_wT"][:, :], t["ps_b"][:, 0:D])
            v.tensor_copy(t["l1_wT"][:, :], t["ps_b"][:, D:2 * D])
            v.drain()
            v.tensor_scalar(w["bk_scaled"][:, :], w["bqkv"][:, 1:2], QK_SCALE, None, ALU.mult).then_inc(t["dve_out"], 1)
            v.wait_ge(t["pe_out"], 2)
            v.tensor_copy(w["l1_wsrc"][:, :], t["ps_c"][:, 0:D])
            v.tensor_copy(w["l1_wdst"][:, :], t["ps_c"][:, D:2 * D])
            v.tensor_copy(t["c0_row"][:, :], t["ps_row"][:, 0:D])
            v.drain()
            v.tensor_scalar(w["neg_row"][:, :], t["c0_row"][:, :], -1.0, None, ALU.mult)
            v.tensor_tensor(w["c_row"][:, :], t["c0_row"][:, :], t["b2_row"][:, :], ALU.add)
            v.drain()
            for j in range(TILES):
                v.tensor_copy(tile(t["c_row4"], j), w["c_row"][:, :])
            v.drain().then_inc(t["dve_out"], 1)
            v.wait_ge(t["pe_out"], 3)
            v.tensor_copy(w["c4"][:, :], t["ps_a"][:, :])
            for j in range(TILES):
                v.tensor_copy(tile(w["l1_b4"], j), t["ps_b"][:, 0:D])
            v.memset(count[1][:, CHUNK - 1:CHUNK], 0.0)
            v.drain()

            def marks(c, k, wait_cols):
                v.wait_ge(dst_sem[k], wait_cols)
                v.tensor_tensor(t["same"][:, :], cur[k][:, :], prev[k][:, :], ALU.is_equal)
                v.drain()
                v.tensor_scalar(w["run_gap"][:, bass.ds(c * CHUNK, CHUNK)], t["same"][:, :], 1.0, -GAP,
                                ALU.subtract, ALU.mult)
                v.tensor_tensor_scan(count[k][:, :], t["same"][:, :], w["ones_wide"][:, :],
                                     count[1 - k][:, CHUNK - 1:CHUNK], ALU.mult, ALU.add)\
                 .then_inc(t["counted"], 1)
                v.wait_ge(t["count_cols"], c + 1)
                v.tensor_scalar(w["rdeg"][:, bass.ds(c * TILES, TILES)], ps_cnt[k][:, 0:TILES], 1.0, None,
                                ALU.max)
                v.drain()

            v.memset(w["ones_wide"][:, :], 1.0)
            v.drain()
            with v.Fori(0, EDGE_CHUNKS // 2) as i:
                c = v.snap(2 * i)
                loads_seen = v.snap((2 * DMA) * i)
                for k in range(2):
                    marks(c + k, k, loads_seen + 2 * DMA)
            v.reciprocal(w["rdeg"][:, :], w["rdeg"][:, :])

        @block.scalar
        def _(a):
            a.wait_ge(t["dve_out"], 1)
            a.activation(t["gelu_b1"][:, :], w["b1"][:, :], ACT.Gelu).then_inc(t["act_out"], 1)

        @block.tensor
        def _(pe):
            pe.wait_ge(t["loaded"], DMA * len(loads))
            pe.wait_ge(t["ident_ready"], 1)
            for j in range(3):
                pe.matmul(t["ps_a"][:, j:j + 1], tile(t["wqkv_raw"], j), t["nin_b"][:, 0:1], start=True, stop=True)
            for j in range(HC):
                pe.matmul(t["ps_a"][:, 4 + j:5 + j], tile(t["w1_raw"], j), t["no_b"][:, 0:1], start=True, stop=True)
            pe.transpose(t["ps_b"][:, 0:D], t["w2l2_raw"][:, :], w["ident"][:, :])
            pe.transpose(t["ps_b"][:, D:2 * D], w["l1_w"][:, :], w["ident"][:, :]).then_inc(t["pe_out"], 1)
            pe.wait_ge(t["dve_out"], 1)
            pe.wait_ge(t["blocks"], 1)
            pe.matmul(t["ps_c"][:, 0:D], t["l1_wT"][:, :], t["block_src"][:, :], start=True, stop=True)
            pe.matmul(t["ps_c"][:, D:2 * D], t["l1_wT"][:, :], t["block_dst"][:, :], start=True, stop=True)
            pe.wait_ge(t["act_out"], 1)
            for j in range(HC):
                last = pe.matmul(t["ps_row"][:, 0:D], t["gelu_b1"][:, j:j + 1], tile(w["w2"], j),
                                 start=j == 0, stop=j == HC - 1)
            last.then_inc(t["pe_out"], 1)
            pe.wait_ge(t["dve_out"], 2)
            pe.matmul(t["ps_a"][:, :], w["ones_row"][:, :], t["c_row4"][:, :], start=True, stop=True)
            pe.matmul(t["ps_b"][:, 0:D], w["ones_row"][:, :], t["l1b_row"][:, :], start=True, stop=True)\
              .then_inc(t["pe_out"], 1)

            with pe.Fori(0, EDGE_CHUNKS // 2) as i:
                c = pe.snap(2 * i)
                for k in range(2):
                    pe.wait_ge(t["counted"], c + (k + 1))
                    for j in range(TILES):
                        last = pe.matmul(ps_cnt[k][:, j:j + 1], tile(count[k], j)[0:1, :],
                                         w["ones_row"][0:1, 0:1], start=True, stop=True)
                    last.then_inc(t["count_cols"], 1)


def start_tables(nc, w, inp, tables, neigh):
    with ExitStack() as ctx:
        t = {"phase": "start"}
        alloc(nc, ctx, t, "x0 x1 y0 y1 zeros", [P, CHUNK])
        alloc(nc, ctx, t, "stats0 stats1", [P, 6 * TILES])
        alloc(nc, ctx, t, "mom0 mom1", [P, 2 * TILES])
        alloc(nc, ctx, t, "lv0 lv1 rs0 rs1", [P, TILES])
        semaphores(nc, ctx, t, "in0 in1 out0 out1 stats_done rstd_done norm_done relu_done z")
        x, y, stats, mom = (t["x0"], t["x1"]), (t["y0"], t["y1"]), (t["stats0"], t["stats1"]), (t["mom0"], t["mom1"])
        lv, rs, s_in, s_out = (t["lv0"], t["lv1"]), (t["rs0"], t["rs1"]), (t["in0"], t["in1"]), (t["out0"], t["out1"])
        src = inp["x"]
        view = lambda tab, c, at=0: tab[bass.ds(c * CHUNK + at, CHUNK), :].rearrange("(p j) d -> p (j d)", p=P)
        block = ctx.enter_context(nc.Block())
        half = lambda c, k: c - k

        @block.sync
        def _(sp):
            def load(c, k, first=False):
                if not first:
                    wait_apart(sp, t["norm_done"], c - 1)
                sp.dma_start(x[k][:, :], view(src, c)).then_inc(s_in[k], DMA)

            def store(c, k):
                wait_apart(sp, t["relu_done"], c + 1)
                sp.dma_start(view(tables, c), y[k][:, :]).then_inc(s_out[k], DMA)
                sp.dma_start(view(tables, c, NP), y[k][:, :]).then_inc(s_out[k], DMA)
                sp.dma_start(view(neigh, c), t["zeros"][:, :]).then_inc(s_out[k], DMA)

            sp.wait_ge(t["z"], 1)
            load(0, 0, True)
            load(1, 1, True)
            with sp.Fori(0, NODE_CHUNKS // 2 - 1) as i:
                c = sp.snap(2 * i)
                for k in range(2):
                    load(c + (2 + k), k)
                    store(c + k, k)
            for k in range(2):
                store(NODE_CHUNKS - 2 + k, k)
            for k in range(2):
                sp.wait_ge(s_out[k], 3 * DMA * (NODE_CHUNKS // 2))

        @block.vector
        def _(v):
            v.memset(t["zeros"][:, :], 0.0).then_inc(t["z"], 1)

            def stats_of(c, k):
                v.wait_ge(s_in[k], half(c, k) * (DMA // 2) + DMA)
                row_stats(v, [tile(x[k], j) for j in range(TILES)], stats[k], mom[k]).then_inc(t["stats_done"], 1)

            def norm(c, k):
                v.wait_ge(t["rstd_done"], c + 1)
                normalise(v, [tile(x[k], j) for j in range(TILES)], [tile(x[k], j) for j in range(TILES)],
                          mom[k], rs[k])
                v.drain()
                if later(c, 2):
                    v.wait_ge(s_out[k], half(c, k) * (3 * DMA // 2))
                v.tensor_scalar(y[k][:, :], x[k][:, :], 0.0, None, ALU.max).then_inc(t["relu_done"], 1)
                v.drain().then_inc(t["norm_done"], 1)

            run_slots(v, NODE_CHUNKS, 4, [(1, norm), (0, stats_of)])

        @block.scalar
        def _(a):
            def rstd(c, k):
                a.wait_ge(t["stats_done"], c + 1)
                inverse_std(a, mom[k], lv[k], rs[k], TILES, w["eps_col"][:, 0:1]).then_inc(t["rstd_done"], 1)

            run_slots(a, NODE_CHUNKS, 4, [(0, log_exp_tables(a)), (0, rstd)])


def attention_rounds(nc, w, tables):
    with ExitStack() as ctx:
        t = {"phase": "rounds"}
        alloc(nc, ctx, t, "gs0 gs1 gd0 gd1 hs0 hs1 xs0 xs1 xd0 xd1 sT0 sT1 dT0 dT1 ks0 ks1 att0 att1 "
                          "z0 z1 u0 u1 r0 r1 ve n30 n31 nT0 nT1 lz rz0 rz1 new0 new1", [P, CHUNK])
        alloc(nc, ctx, t, "hd_ring", [P, RING * CHUNK])
        alloc(nc, ctx, t, "m0 m1", [P, 1 + CHUNK])
        alloc(nc, ctx, t, "d0 d1", [P, 2 * CHUNK])
        alloc(nc, ctx, t, "hid0 hid1", [P, HC * CHUNK])
        alloc(nc, ctx, t, "st1 st2 st3", [P, 12 * TILES])
        alloc(nc, ctx, t, "ma0 ma1 mb0 mb1 mc0 mc1", [P, 4 * TILES])
        alloc(nc, ctx, t, "lv1 lv2 lv3 ra0 ra1 rb0 rb1 rc0 rc1 nb0 nb1 nc0 nc1", [P, 2 * TILES])
        alloc(nc, ctx, t, "idx_read0 idx_read1", [P, 2 * TILES], I32)
        alloc(nc, ctx, t, "idx_end0 idx_end1 read_half write_half half_step", [P, TILES], I32)
        alloc(nc, ctx, t, "ps_s ps_d ps_q ps_k ps_v ps_r ps_hid ps_y", [P, CHUNK], F32, "psum")
        semaphores(nc, ctx, t,
                   "halves idx_made end_made gathered0 gathered1 rows_in stats1 rstd1 stats2 rstd2 shift2 "
                   "x_ready transposed sd_ready k_done qv_done k_ready arg_ready exp_done v_used "
                   "zu_ready rz_ready r_ready r_rows stats3 rstd3 shift3 n3_ready n3_cols nT_ready hid_done "
                   "gelu_done y_done new_ready scattered0 scattered1 round_set")
        two = lambda name: (t[name + "0"], t[name + "1"])
        gs, gd, hs, xs, xd, sT, dT, ks, att = (two(n) for n in "gs gd hs xs xd sT dT ks att".split())
        z, u, r, n3, nT, rz, new, m, d, hid = (two(n) for n in "z u r n3 nT rz new m d hid".split())
        ma, mb, mc, ra, rb, rc, shift2, shift3 = (two(n) for n in "ma mb mc ra rb rc nb nc".split())
        idx_read, idx_end, gathered, scattered = (two(n) for n in "idx_read idx_end gathered scattered".split())
        first = 6
        tiles = range(TILES)
        hid_bank = (t["ps_hid"], t["ps_d"])

        def chunks_before_up(base, c):
            return base + (min(c + 3, EDGE_CHUNKS) if isinstance(c, int) else c + 3)

        def ring(g, j=0, width=D):
            return t["hd_ring"][:, bass.ds((g & (RING - 1)) * CHUNK + j * D, width)]

        block = ctx.enter_context(nc.Block())

        @block.gpsimd
        def _(pool):
            pool.sem_inc(t["rows_in"], 2)
            pool.memset(t["read_half"][:, :], 0)
            pool.memset(t["write_half"][:, :], NP)
            pool.memset(t["half_step"][:, :], NP).then_inc(t["halves"], 1)
            pool.wait_ge(t["halves"], 1)
            with pool.Fori(0, ROUNDS) as rnd:
                base = pool.snap(rnd * EDGE_CHUNKS)
                wait_apart(pool, t["round_set"], rnd + 1)

                def gather(c, k):
                    g = base + c
                    pool.wait_ge(t["rows_in"], g + 1)
                    cols = bass.ds(c * TILES, TILES)
                    pool.tensor_tensor(idx_read[k][:, 0:TILES], w["src_idx"][:, cols], t["read_half"][:, :], ALU.add)
                    pool.tensor_tensor(idx_read[k][:, TILES:2 * TILES], w["dst_idx"][:, cols], t["read_half"][:, :],
                                       ALU.add).then_inc(t["idx_made"], 1)
                    wait_apart(pool, t["idx_made"], g + 1)
                    for rows, at in ((gs[k], 0), (gd[k], TILES)):
                        for j in tiles:
                            pool.indirect_dma_start(
                                out=tile(rows, j), out_offset=None, in_=tables[:, :],
                                in_offset=AX(ap=idx_read[k][:, at + j:at + j + 1], axis=0))\
                                .then_inc(gathered[k], DMA)

                def add_lc(c, k):
                    g = base + c
                    if later(c, 2):
                        pool.wait_ge(t["stats2"], g - 1)
                    pool.wait_ge(gathered[k], (g - k) * (DMA * TILES) + 2 * TILES * DMA)
                    pool.tensor_tensor(hs[k][:, :], gs[k][:, :], w["lc4"][:, :], ALU.add)
                    pool.tensor_tensor(ring(g, 0, CHUNK), gd[k][:, :], w["lc4"][:, :], ALU.add).then_inc(t["rows_in"], 1)

                def scatter(c, k):
                    g = base + c
                    pool.wait_ge(t["new_ready"], g + 1)
                    if later(c, 2):
                        pool.wait_ge(scattered[k], (g - k) * (DMA * TILES // 2))
                    pool.tensor_tensor(idx_end[k][:, :], w["end_idx"][:, bass.ds(c * TILES, TILES)],
                                       t["write_half"][:, :], ALU.add).then_inc(t["end_made"], 1)
                    wait_apart(pool, t["end_made"], g + 1)
                    for j in tiles:
                        pool.indirect_dma_start(
                            out=tables[:, :], out_offset=AX(ap=idx_end[k][:, j:j + 1], axis=0),
                            in_=tile(new[k], j), in_offset=None, bounds_check=2 * NP - 1,
                            oob_is_err=False).then_inc(scattered[k], DMA)

                run_slots(pool, EDGE_CHUNKS, first, [(0, gather), (5, scatter), (0, add_lc)])
                for k in range(2):
                    pool.wait_ge(scattered[k], (base + EDGE_CHUNKS) * (DMA * TILES // 2))
                for half in (t["read_half"], t["write_half"]):
                    last = pool.tensor_tensor(half[:, :], t["half_step"][:, :], half[:, :], ALU.subtract)
                last.then_inc(t["halves"], 1)
                wait_apart(pool, t["halves"], rnd + 2)

        @block.vector
        def _(v):
            for k in range(2):
                for carry in (z[k], u[k]):
                    v.memset(carry[:, CHUNK - 1:CHUNK], 0.0)
                v.memset(m[k][:, CHUNK:CHUNK + 1], 0.0)
            v.sem_inc(t["transposed"], 2)
            v.sem_inc(t["round_set"], 1)
            v.drain()
            with v.Fori(0, ROUNDS) as rnd:
                base = v.snap(rnd * EDGE_CHUNKS)

                def stats_1(c, k):
                    g = base + c
                    v.wait_ge(t["rows_in"], g + 3)
                    row_stats(v, [tile(hs[k], j) for j in tiles] + [ring(g, j) for j in tiles],
                              t["st1"], ma[k]).then_inc(t["stats1"], 1)

                def stats_2(c, k):
                    g = base + c
                    v.wait_ge(t["rstd1"], g + 1)
                    v.wait_ge(t["transposed"], g + 1)
                    rows = [tile(hs[k], j) for j in tiles] + [ring(g, j) for j in tiles]
                    outs = [tile(xs[k], j) for j in tiles] + [tile(xd[k], j) for j in tiles]
                    for j, (o, h) in enumerate(zip(outs, rows)):
                        v.scalar_tensor_tensor(o, h, ma[k][:, 2 * j:2 * j + 1], w["norm_w"][:, :],
                                               ALU.subtract, ALU.mult)
                    v.drain()
                    for j, o in enumerate(outs):
                        v.scalar_tensor_tensor(o, o, ra[k][:, j:j + 1], w["norm_b"][:, :], ALU.mult, ALU.add)
                    v.drain()
                    row_stats(v, outs, t["st2"], mb[k]).then_inc(t["stats2"], 1)

                def shift_2(c, k):
                    v.wait_ge(t["rstd2"], base + c + 1)
                    shift_of(v, shift2[k], mb[k], rb[k], 2 * TILES).then_inc(t["shift2"], 1)

                def running_max(c, k):
                    g = base + c
                    v.wait_ge(t["k_ready"], g + 1)
                    v.wait_ge(t["qv_done"], g + 1)
                    v.scalar_tensor_tensor(att[k][:, :], t["ps_q"][:, :], w["bqkv"][:, 0:1], ks[k][:, :],
                                           ALU.add, ALU.mult)
                    v.tensor_copy(m[k][:, 0:1], m[1 - k][:, CHUNK:CHUNK + 1])
                    v.drain()
                    gap = w["run_gap"][:, bass.ds(c * CHUNK, CHUNK)]
                    v.tensor_tensor_scan(m[k][:, 1:1 + CHUNK], gap, att[k][:, :],
                                         m[1 - k][:, CHUNK:CHUNK + 1], ALU.add, ALU.max)
                    v.drain()
                    v.tensor_tensor(d[k][:, 0:CHUNK], m[k][:, 0:CHUNK], m[k][:, 1:1 + CHUNK], ALU.subtract)
                    v.tensor_tensor(d[k][:, CHUNK:2 * CHUNK], att[k][:, :], m[k][:, 1:1 + CHUNK], ALU.subtract)
                    v.drain()
                    v.tensor_tensor(d[k][:, 0:CHUNK], d[k][:, 0:CHUNK], gap, ALU.add).then_inc(t["arg_ready"], 1)

                def run_sums(c, k):
                    v.wait_ge(t["exp_done"], base + c + 1)
                    decay, e = d[k][:, 0:CHUNK], d[k][:, CHUNK:2 * CHUNK]
                    v.scalar_tensor_tensor(t["ve"][:, :], t["ps_v"][:, :], w["bqkv"][:, 2:3], e, ALU.add, ALU.mult)\
                     .then_inc(t["v_used"], 1)
                    v.tensor_tensor_scan(z[k][:, :], decay, e, z[1 - k][:, CHUNK - 1:CHUNK], ALU.mult, ALU.add)
                    v.drain()
                    v.tensor_tensor_scan(u[k][:, :], decay, t["ve"][:, :], u[1 - k][:, CHUNK - 1:CHUNK],
                                         ALU.mult, ALU.add).then_inc(t["zu_ready"], 1)

                def softmax_out(c, k):
                    v.wait_ge(t["rz_ready"], base + c + 1)
                    v.tensor_tensor(r[k][:, :], u[k][:, :], rz[k][:, :], ALU.mult).then_inc(t["r_ready"], 1)

                def stats_3(c, k):
                    v.wait_ge(t["r_rows"], base + c + 1)
                    row_stats(v, [tile(t["ps_r"], j) for j in tiles], t["st3"], mc[k]).then_inc(t["stats3"], 1)

                def shift_3(c, k):
                    v.wait_ge(t["rstd3"], base + c + 1)
                    shift_of(v, shift3[k], mc[k], rc[k], TILES).then_inc(t["shift3"], 1)

                def new_rows(c, k):
                    g = base + c
                    v.wait_ge(t["y_done"], g + 1)
                    if later(c, 2):
                        v.wait_ge(scattered[k], (g - k) * (DMA * TILES // 2))
                    v.tensor_tensor(new[k][:, :], t["ps_y"][:, :], ring(g, 0, CHUNK), ALU.add)\
                     .then_inc(t["new_ready"], 1)

                run_slots(v, EDGE_CHUNKS, first, [
                    (5, new_rows), (3, run_sums), (4, shift_3), (1, stats_2), (3, softmax_out),
                    (2, running_max), (1, shift_2), (3, stats_3), (0, stats_1)])
                v.tensor_tensor(w["lc4"][:, :], w["lc4"][:, :], w["c4"][:, :], ALU.add)
                v.tensor_tensor(w["neg_row"][:, :], w["neg_row"][:, :], w["c_row"][:, :], ALU.subtract)
                v.drain().then_inc(t["round_set"], 1)

        @block.scalar
        def _(a):
            eps = w["eps_col"][:, 0:1]
            with a.Fori(0, ROUNDS) as rnd:
                base = a.snap(rnd * EDGE_CHUNKS)

                def gelus(c, k):
                    g4 = (base + c) * HC
                    for j in range(HC):
                        a.wait_ge(t["hid_done"], g4 + (j + 1))
                        a.activation(tile(hid[k], j, CHUNK), hid_bank[j % 2][:, :], ACT.Gelu, bias=w["b1"][:, j:j + 1])\
                         .then_inc(t["gelu_done"], 1)

                def gelu_and_log_exp_tables(c, k):
                    gelus(c, k)
                    a.preload_act_table_set("natural_log_exp_and_others")

                def exps(c, k):
                    a.wait_ge(t["arg_ready"], base + c + 1)
                    a.activation(d[k][:, :], d[k][:, :], ACT.Exp).then_inc(t["exp_done"], 1)

                def scaled_k(c, k):
                    a.wait_ge(t["k_done"], base + c + 1)
                    a.activation(ks[k][:, :], t["ps_k"][:, :], ACT.Identity, bias=w["bk_scaled"][:, 0:1],
                                 scale=QK_SCALE).then_inc(t["k_ready"], 1)

                def rstd(ready, mom, log_var, out, n, done):
                    def body(c, k):
                        a.wait_ge(ready, base + c + 1)
                        inverse_std(a, mom[k], log_var, out[k], n, eps).then_inc(done, 1)
                    return body

                def inverse_z(c, k):
                    a.wait_ge(t["zu_ready"], base + c + 1)
                    a.activation(t["lz"][:, :], z[k][:, :], ACT.Ln)
                    a.drain()
                    a.activation(rz[k][:, :], t["lz"][:, :], ACT.Exp, scale=-1.0).then_inc(t["rz_ready"], 1)

                def n3_to_sbuf(c, k):
                    a.wait_ge(t["n3_cols"], base + c + 1)
                    a.activation(nT[k][:, :], t["ps_r"][:, :], ACT.Copy).then_inc(t["nT_ready"], 1)

                def sd_to_sbuf(c, k):
                    a.wait_ge(t["transposed"], base + c + 3)
                    a.activation(sT[k][:, :], t["ps_s"][:, :], ACT.Copy)
                    a.activation(dT[k][:, :], t["ps_d"][:, :], ACT.Copy).then_inc(t["sd_ready"], 1)

                def norm_2(c, k):
                    a.wait_ge(t["shift2"], base + c + 1)
                    outs = [tile(xs[k], j) for j in tiles] + [tile(xd[k], j) for j in tiles]
                    scale_and_shift(a, outs, outs, rb[k], shift2[k]).then_inc(t["x_ready"], 1)

                def norm_3(c, k):
                    a.wait_ge(t["shift3"], base + c + 1)
                    scale_and_shift(a, [tile(n3[k], j) for j in tiles], [tile(t["ps_r"], j) for j in tiles],
                                    rc[k], shift3[k]).then_inc(t["n3_ready"], 1)

                rstd_1 = rstd(t["stats1"], ma, t["lv1"], ra, 2 * TILES, t["rstd1"])
                rstd_2 = rstd(t["stats2"], mb, t["lv2"], rb, 2 * TILES, t["rstd2"])
                rstd_3 = rstd(t["stats3"], mc, t["lv3"], rc, TILES, t["rstd3"])
                run_slots(a, EDGE_CHUNKS, first, [
                    (0, rstd_1), (2, inverse_z), (3, norm_3), (3, n3_to_sbuf), (1, scaled_k),
                    (3, gelu_and_log_exp_tables), (0, rstd_2), (0, norm_2), (1, exps), (2, rstd_3),
                    (0, sd_to_sbuf)])

        @block.tensor
        def _(pe):
            with pe.Fori(0, ROUNDS) as rnd:
                base = pe.snap(rnd * EDGE_CHUNKS)
                pe.wait_ge(t["round_set"], rnd + 1)

                def up(c, k):
                    pe.wait_ge(t["nT_ready"], base + c + 1)
                    g4 = (base + c) * HC
                    for j in range(HC):
                        if j == 1:
                            pe.wait_ge(t["sd_ready"], chunks_before_up(base, c))
                        if later(c, 1) or j > 1:
                            pe.wait_ge(t["gelu_done"], g4 + (j - 1 if j > 1 else 0))
                        pe.matmul(hid_bank[j % 2][:, :], tile(w["w1"], j), nT[k][:, :], start=True, stop=True)\
                          .then_inc(t["hid_done"], 1)

                def r_to_rows(c, k):
                    g = base + c
                    pe.wait_ge(t["r_ready"], g + 1)
                    if later(c, 1):
                        pe.wait_ge(t["nT_ready"], g)
                    for j in tiles:
                        last = pe.transpose(tile(t["ps_r"], j), tile(r[k], j), w["ident"][:, :])
                    last.then_inc(t["r_rows"], 1)

                def qkv(c, k):
                    g = base + c
                    pe.wait_ge(t["sd_ready"], g + 1)
                    if later(c, 1):
                        pe.wait_ge(t["arg_ready"], g)
                    pe.matmul(t["ps_k"][:, :], tile(w["wqkv"], 1), dT[k][:, :], start=True, stop=True).then_inc(t["k_done"], 1)
                    pe.matmul(t["ps_q"][:, :], tile(w["wqkv"], 0), sT[k][:, :], start=True, stop=True)
                    if later(c, 1):
                        pe.wait_ge(t["v_used"], g)
                    pe.matmul(t["ps_v"][:, :], tile(w["wqkv"], 2), sT[k][:, :], start=True, stop=True).then_inc(t["qv_done"], 1)

                def down(c, k):
                    g = base + c
                    pe.wait_ge(t["gelu_done"], (g + 1) * HC)
                    if later(c, 1):
                        pe.wait_ge(t["new_ready"], g)
                    for j in tiles:
                        pe.matmul(tile(t["ps_y"], j), w["ones_row"][:, :], w["neg_row"][:, :], start=True, stop=False)
                        for i in range(HC):
                            last = pe.matmul(tile(t["ps_y"], j), hid[k][:, i * CHUNK + j * P:i * CHUNK + (j + 1) * P],
                                             tile(w["w2"], i), start=False, stop=i == HC - 1)
                    last.then_inc(t["y_done"], 1)

                def x_to_cols(c, k):
                    g = base + c
                    pe.wait_ge(t["x_ready"], g + 1)
                    if later(c, 1):
                        pe.wait_ge(t["sd_ready"], g)
                    if later(c, 3):
                        pe.wait_ge(t["gelu_done"], (g - 2) * HC)
                    for bank, rows in ((t["ps_s"], xs[k]), (t["ps_d"], xd[k])):
                        for j in tiles:
                            last = pe.transpose(tile(bank, j), tile(rows, j), w["ident"][:, :])
                    last.then_inc(t["transposed"], 1)

                def n3_to_cols(c, k):
                    pe.wait_ge(t["n3_ready"], base + c + 1)
                    for j in tiles:
                        last = pe.transpose(tile(t["ps_r"], j), tile(n3[k], j), w["ident"][:, :])
                    last.then_inc(t["n3_cols"], 1)

                run_slots(pe, EDGE_CHUNKS, first, [
                    (5, down), (2, x_to_cols), (2, qkv), (4, n3_to_cols), (4, up), (3, r_to_rows)])


def nodes(tab, c, at=0):
    return tab[bass.ds(c * CHUNK + at, CHUNK), :].rearrange("(p j) d -> p (j d)", p=P)


def close_rounds(nc, w, inp, tables, x1_tab, x2_tab):
    with ExitStack() as ctx:
        t = {"phase": "close"}
        alloc(nc, ctx, t, "x0 x1 h0 h1 a0 a1 b0 b1", [P, CHUNK])
        semaphores(nc, ctx, t, "in0 in1 out0 out1 added")
        x, h, a, b = (t["x0"], t["x1"]), (t["h0"], t["h1"]), (t["a0"], t["a1"]), (t["b0"], t["b1"])
        s_in, s_out = (t["in0"], t["in1"]), (t["out0"], t["out1"])
        block = ctx.enter_context(nc.Block())

        @block.sync
        def _(sp):
            def load(c, k):
                sp.dma_start(x[k][:, :], nodes(inp["x"], c)).then_inc(s_in[k], DMA)
                sp.dma_start(h[k][:, :], nodes(tables, c, NP)).then_inc(s_in[k], DMA)

            def store(c, k):
                wait_apart(sp, t["added"], c + 1)
                sp.dma_start(nodes(x1_tab, c), a[k][:, :]).then_inc(s_out[k], DMA)
                sp.dma_start(nodes(x2_tab, c), b[k][:, :]).then_inc(s_out[k], DMA)

            run_slots(sp, NODE_CHUNKS, 4, [(2, store), (0, load)])
            for k in range(2):
                sp.wait_ge(s_out[k], 2 * DMA * (NODE_CHUNKS // 2))

        @block.vector
        def _(v):
            def add(c, k):
                v.wait_ge(s_in[k], (c - k) * DMA + 2 * DMA)
                v.tensor_tensor(x[k][:, :], x[k][:, :], h[k][:, :], ALU.add)
                v.drain()
                if later(c, 2):
                    v.wait_ge(s_out[k], (c - k) * DMA)
                v.tensor_tensor(a[k][:, :], x[k][:, :], w["lc4"][:, :], ALU.add)
                v.drain()
                v.tensor_tensor(b[k][:, :], a[k][:, :], w["l1_b4"][:, :], ALU.add).then_inc(t["added"], 1)

            run_slots(v, NODE_CHUNKS, 4, [(1, add)])


def graph_attention(nc, w, x1_tab, x2_tab):
    with ExitStack() as ctx:
        t = {"phase": "gat"}
        alloc(nc, ctx, t, "gs0 gs1 gd0 gd1 xs0 xs1 xd0 xd1 sT0 sT1 dT0 dT1 att0 att1 raw "
                          "z0 z1 zc0 zc1 u0 u1 r0 r1 ve lz rz0 rz1 new0 new1", [P, CHUNK])
        alloc(nc, ctx, t, "res_ring", [P, RING * CHUNK])
        alloc(nc, ctx, t, "m0 m1", [P, 1 + CHUNK])
        alloc(nc, ctx, t, "d0 d1", [P, 2 * CHUNK])
        alloc(nc, ctx, t, "st", [P, 12 * TILES])
        alloc(nc, ctx, t, "mom0 mom1", [P, 4 * TILES])
        alloc(nc, ctx, t, "lv rs0 rs1", [P, 2 * TILES])
        alloc(nc, ctx, t, "idx_read0 idx_read1", [P, 2 * TILES], I32)
        alloc(nc, ctx, t, "idx_end0 idx_end1", [P, TILES], I32)
        alloc(nc, ctx, t, "ps_s ps_d ps_logit ps_v ps_r", [P, CHUNK], F32, "psum")
        semaphores(nc, ctx, t,
                   "idx_made end_made gathered0 gathered1 rows_free stats rstd x_ready transposed sd_ready "
                   "logit_done v_done raw_ready arg_ready exp_done v_used zu_ready rz_ready r_ready r_rows "
                   "new_ready scattered0 scattered1")
        two = lambda name: (t[name + "0"], t[name + "1"])
        gs, gd, xs, xd, sT, dT, att, z, zc, u = (two(n) for n in "gs gd xs xd sT dT att z zc u".split())
        r, rz, new, m, d, mom, rs = (two(n) for n in "r rz new m d mom rs".split())
        idx_read, idx_end, gathered, scattered = (two(n) for n in "idx_read idx_end gathered scattered".split())
        first = 8
        tiles = range(TILES)
        block = ctx.enter_context(nc.Block())

        @block.gpsimd
        def _(pool):
            def gather(c, k):
                pool.wait_ge(t["rows_free"], c + 1)
                cols = bass.ds(c * TILES, TILES)
                pool.tensor_copy(idx_read[k][:, 0:TILES], w["src_idx"][:, cols])
                pool.tensor_copy(idx_read[k][:, TILES:2 * TILES], w["dst_idx"][:, cols]).then_inc(t["idx_made"], 1)
                wait_apart(pool, t["idx_made"], c + 1)
                for rows, at in ((gs[k], 0), (gd[k], TILES)):
                    for j in tiles:
                        pool.indirect_dma_start(
                            out=tile(rows, j), out_offset=None, in_=x1_tab[:, :],
                            in_offset=AX(ap=idx_read[k][:, at + j:at + j + 1], axis=0)).then_inc(gathered[k], DMA)

            def scatter(c, k):
                pool.wait_ge(t["new_ready"], c + 1)
                if later(c, 2):
                    pool.wait_ge(scattered[k], (c - k) * (DMA * TILES // 2))
                pool.tensor_copy(idx_end[k][:, :], w["end_idx"][:, bass.ds(c * TILES, TILES)]).then_inc(t["end_made"], 1)
                wait_apart(pool, t["end_made"], c + 1)
                for j in tiles:
                    pool.indirect_dma_start(
                        out=x2_tab[:, :], out_offset=AX(ap=idx_end[k][:, j:j + 1], axis=0), in_=tile(new[k], j),
                        in_offset=None, bounds_check=NP - 1, oob_is_err=False).then_inc(scattered[k], DMA)

            run_slots(pool, EDGE_CHUNKS, first, [(0, gather), (5, scatter)])
            for k in range(2):
                pool.wait_ge(scattered[k], EDGE_CHUNKS * (DMA * TILES // 2))

        @block.vector
        def _(v):
            for k in range(2):
                for carry in (z[k], u[k]):
                    v.memset(carry[:, CHUNK - 1:CHUNK], 0.0)
                v.memset(m[k][:, CHUNK:CHUNK + 1], 0.0)
            v.sem_inc(t["rows_free"], 2)
            v.sem_inc(t["transposed"], 2)
            v.drain()

            def ring(c):
                return t["res_ring"][:, bass.ds((c & (RING - 1)) * CHUNK, CHUNK)]

            def stats(c, k):
                v.wait_ge(gathered[k], (c - k) * (DMA * TILES) + 2 * TILES * DMA)
                v.tensor_tensor(ring(c), gd[k][:, :], w["l1_b4"][:, :], ALU.add)
                row_stats(v, [tile(g[k], j) for g in (gs, gd) for j in tiles], t["st"], mom[k]).then_inc(t["stats"], 1)

            def norm(c, k):
                v.wait_ge(t["rstd"], c + 1)
                v.wait_ge(t["transposed"], c + 1)
                normalise(v, [tile(g[k], j) for g in (xs, xd) for j in tiles],
                          [tile(g[k], j) for g in (gs, gd) for j in tiles], mom[k], rs[k]).then_inc(t["x_ready"], 1)
                v.drain().then_inc(t["rows_free"], 1)

            def running_max(c, k):
                v.wait_ge(t["raw_ready"], c + 1)
                v.scalar_tensor_tensor(att[k][:, :], t["raw"][:, :], 0.2, t["raw"][:, :], ALU.mult, ALU.max)
                v.tensor_copy(m[k][:, 0:1], m[1 - k][:, CHUNK:CHUNK + 1])
                v.drain()
                gap = w["run_gap"][:, bass.ds(c * CHUNK, CHUNK)]
                v.tensor_tensor_scan(m[k][:, 1:1 + CHUNK], gap, att[k][:, :],
                                     m[1 - k][:, CHUNK:CHUNK + 1], ALU.add, ALU.max)
                v.drain()
                v.tensor_tensor(d[k][:, 0:CHUNK], m[k][:, 0:CHUNK], m[k][:, 1:1 + CHUNK], ALU.subtract)
                v.tensor_tensor(d[k][:, CHUNK:2 * CHUNK], att[k][:, :], m[k][:, 1:1 + CHUNK], ALU.subtract)
                v.drain()
                v.tensor_tensor(d[k][:, 0:CHUNK], d[k][:, 0:CHUNK], gap, ALU.add).then_inc(t["arg_ready"], 1)

            def run_sums(c, k):
                v.wait_ge(t["exp_done"], c + 1)
                v.wait_ge(t["v_done"], c + 1)
                decay, e = d[k][:, 0:CHUNK], d[k][:, CHUNK:2 * CHUNK]
                v.tensor_tensor(t["ve"][:, :], t["ps_v"][:, :], e, ALU.mult).then_inc(t["v_used"], 1)
                v.tensor_tensor_scan(z[k][:, :], decay, e, z[1 - k][:, CHUNK - 1:CHUNK], ALU.mult, ALU.add)
                v.drain()
                v.tensor_scalar(zc[k][:, :], z[k][:, :], 1e-9, None, ALU.max)
                v.tensor_tensor_scan(u[k][:, :], decay, t["ve"][:, :], u[1 - k][:, CHUNK - 1:CHUNK],
                                     ALU.mult, ALU.add).then_inc(t["zu_ready"], 1)

            def softmax_out(c, k):
                v.wait_ge(t["rz_ready"], c + 1)
                v.tensor_tensor(r[k][:, :], u[k][:, :], rz[k][:, :], ALU.mult).then_inc(t["r_ready"], 1)

            def new_rows(c, k):
                v.wait_ge(t["r_rows"], c + 1)
                if later(c, 2):
                    v.wait_ge(scattered[k], (c - k) * (DMA * TILES // 2))
                v.tensor_tensor(new[k][:, :], t["ps_r"][:, :], ring(c), ALU.add).then_inc(t["new_ready"], 1)

            run_slots(v, EDGE_CHUNKS, first, [(5, softmax_out), (2, norm), (4, run_sums), (3, running_max),
                                              (5, new_rows), (1, stats)])

        @block.scalar
        def _(a):
            def exps(c, k):
                a.wait_ge(t["arg_ready"], c + 1)
                a.activation(d[k][:, :], d[k][:, :], ACT.Exp).then_inc(t["exp_done"], 1)

            def logits(c, k):
                a.wait_ge(t["logit_done"], c + 1)
                a.activation(t["raw"][:, :], t["ps_logit"][:, :], ACT.Copy).then_inc(t["raw_ready"], 1)

            def inverse_z(c, k):
                a.wait_ge(t["zu_ready"], c + 1)
                a.activation(t["lz"][:, :], zc[k][:, :], ACT.Ln)
                a.drain()
                a.activation(rz[k][:, :], t["lz"][:, :], ACT.Exp, scale=-1.0).then_inc(t["rz_ready"], 1)

            def sd_to_sbuf(c, k):
                a.wait_ge(t["transposed"], c + 3)
                a.activation(sT[k][:, :], t["ps_s"][:, :], ACT.Relu)
                a.activation(dT[k][:, :], t["ps_d"][:, :], ACT.Relu).then_inc(t["sd_ready"], 1)

            def rstd(c, k):
                a.wait_ge(t["stats"], c + 1)
                inverse_std(a, mom[k], t["lv"], rs[k], 2 * TILES, w["eps_col"][:, 0:1]).then_inc(t["rstd"], 1)

            run_slots(a, EDGE_CHUNKS, first, [(2, log_exp_tables(a)), (4, exps), (3, logits), (4, inverse_z), (2, sd_to_sbuf), (1, rstd)])

        @block.tensor
        def _(pe):
            def r_to_rows(c, k):
                pe.wait_ge(t["r_ready"], c + 1)
                if later(c, 1):
                    pe.wait_ge(t["new_ready"], c)
                for j in tiles:
                    last = pe.transpose(tile(t["ps_r"], j), tile(r[k], j), w["ident"][:, :])
                last.then_inc(t["r_rows"], 1)

            def project(c, k):
                pe.wait_ge(t["sd_ready"], c + 1)
                if later(c, 1):
                    pe.wait_ge(t["raw_ready"], c)
                pe.matmul(t["ps_logit"][:, :], w["l1_wsrc"][:, :], sT[k][:, :], start=True, stop=False)
                pe.matmul(t["ps_logit"][:, :], w["l1_wdst"][:, :], dT[k][:, :], start=False, stop=True).then_inc(t["logit_done"], 1)
                if later(c, 1):
                    pe.wait_ge(t["v_used"], c)
                pe.matmul(t["ps_v"][:, :], w["l1_w"][:, :], sT[k][:, :], start=True, stop=True).then_inc(t["v_done"], 1)

            def x_to_cols(c, k):
                pe.wait_ge(t["x_ready"], c + 1)
                if later(c, 1):
                    pe.wait_ge(t["sd_ready"], c)
                for bank, rows in ((t["ps_s"], xs[k]), (t["ps_d"], xd[k])):
                    for j in tiles:
                        last = pe.transpose(tile(bank, j), tile(rows, j), w["ident"][:, :])
                last.then_inc(t["transposed"], 1)

            run_slots(pe, EDGE_CHUNKS, first, [(5, r_to_rows), (3, project), (2, x_to_cols)])


def average_neighbours(nc, w, name, x_tab, weight, neigh):
    with ExitStack() as ctx:
        t = {"phase": name}
        alloc(nc, ctx, t, "gs0 gs1 xs0 xs1 sT0 sT1 same0 same1 sum0 sum1 new0 new1", [P, CHUNK])
        alloc(nc, ctx, t, "st", [P, 6 * TILES])
        alloc(nc, ctx, t, "mom0 mom1", [P, 2 * TILES])
        alloc(nc, ctx, t, "lv rs0 rs1", [P, TILES])
        alloc(nc, ctx, t, "idx_read0 idx_read1 idx_end0 idx_end1", [P, TILES], I32)
        alloc(nc, ctx, t, "ps_s ps_o", [P, CHUNK], F32, "psum")
        semaphores(nc, ctx, t, "idx_made end_made gathered0 gathered1 rows_free stats rstd x_ready "
                               "transposed s_ready sum_ready out_done new_ready scattered0 scattered1")
        two = lambda name: (t[name + "0"], t[name + "1"])
        gs, xs, sT, same, total, new, mom, rs = (two(n) for n in "gs xs sT same sum new mom rs".split())
        idx_read, idx_end, gathered, scattered = (two(n) for n in "idx_read idx_end gathered scattered".split())
        first = 6
        tiles = range(TILES)
        block = ctx.enter_context(nc.Block())

        @block.gpsimd
        def _(pool):
            def gather(c, k):
                pool.wait_ge(t["rows_free"], c + 1)
                pool.tensor_copy(idx_read[k][:, :], w["src_idx"][:, bass.ds(c * TILES, TILES)]).then_inc(t["idx_made"], 1)
                wait_apart(pool, t["idx_made"], c + 1)
                for j in tiles:
                    pool.indirect_dma_start(out=tile(gs[k], j), out_offset=None, in_=x_tab[:, :],
                                            in_offset=AX(ap=idx_read[k][:, j:j + 1], axis=0)).then_inc(gathered[k], DMA)

            def scatter(c, k):
                pool.wait_ge(t["new_ready"], c + 1)
                if later(c, 2):
                    pool.wait_ge(scattered[k], (c - k) * (DMA * TILES // 2))
                pool.tensor_copy(idx_end[k][:, :], w["end_idx"][:, bass.ds(c * TILES, TILES)]).then_inc(t["end_made"], 1)
                wait_apart(pool, t["end_made"], c + 1)
                for j in tiles:
                    pool.indirect_dma_start(
                        out=neigh[:, :], out_offset=AX(ap=idx_end[k][:, j:j + 1], axis=0), in_=tile(new[k], j),
                        in_offset=None, bounds_check=NP - 1, oob_is_err=False).then_inc(scattered[k], DMA)

            run_slots(pool, EDGE_CHUNKS, first, [(0, gather), (4, scatter)])
            for k in range(2):
                pool.wait_ge(scattered[k], EDGE_CHUNKS * (DMA * TILES // 2))

        @block.vector
        def _(v):
            for k in range(2):
                v.memset(total[k][:, CHUNK - 1:CHUNK], 0.0)
            v.sem_inc(t["rows_free"], 2)
            v.sem_inc(t["transposed"], 2)
            v.drain()

            def stats(c, k):
                v.wait_ge(gathered[k], (c - k) * (DMA * TILES // 2) + TILES * DMA)
                row_stats(v, [tile(gs[k], j) for j in tiles], t["st"], mom[k]).then_inc(t["stats"], 1)

            def norm(c, k):
                v.wait_ge(t["rstd"], c + 1)
                v.wait_ge(t["transposed"], c + 1)
                normalise(v, [tile(xs[k], j) for j in tiles], [tile(gs[k], j) for j in tiles],
                          mom[k], rs[k]).then_inc(t["x_ready"], 1)
                v.drain().then_inc(t["rows_free"], 1)

            def run_sum(c, k):
                v.tensor_scalar(same[k][:, :], w["run_gap"][:, bass.ds(c * CHUNK, CHUNK)], -1.0 / GAP, 1.0,
                                ALU.mult, ALU.add)
                v.drain()
                v.wait_ge(t["s_ready"], c + 1)
                v.tensor_tensor_scan(total[k][:, :], same[k][:, :], sT[k][:, :],
                                     total[1 - k][:, CHUNK - 1:CHUNK], ALU.mult, ALU.add).then_inc(t["sum_ready"], 1)
                v.drain()

            def new_rows(c, k):
                v.wait_ge(t["out_done"], c + 1)
                if later(c, 2):
                    v.wait_ge(scattered[k], (c - k) * (DMA * TILES // 2))
                for j in tiles:
                    last = v.tensor_scalar(tile(new[k], j), tile(t["ps_o"], j), w["rdeg"][:, bass.ds(c * TILES + j, 1)],
                                           None, ALU.mult)
                last.then_inc(t["new_ready"], 1)

            run_slots(v, EDGE_CHUNKS, first, [(4, new_rows), (3, run_sum), (2, norm), (1, stats)])

        @block.scalar
        def _(a):
            def to_sbuf(c, k):
                a.wait_ge(t["transposed"], c + 3)
                a.activation(sT[k][:, :], t["ps_s"][:, :], ACT.Relu).then_inc(t["s_ready"], 1)

            def rstd(c, k):
                a.wait_ge(t["stats"], c + 1)
                inverse_std(a, mom[k], t["lv"], rs[k], TILES, w["eps_col"][:, 0:1]).then_inc(t["rstd"], 1)

            run_slots(a, EDGE_CHUNKS, first, [(0, log_exp_tables(a)), (2, to_sbuf), (1, rstd)])

        @block.tensor
        def _(pe):
            def project(c, k):
                pe.wait_ge(t["sum_ready"], c + 1)
                if later(c, 1):
                    pe.wait_ge(t["new_ready"], c)
                for j in tiles:
                    last = pe.matmul(tile(t["ps_o"], j), tile(total[k], j), weight[:, :], start=True, stop=True)
                last.then_inc(t["out_done"], 1)

            def x_to_cols(c, k):
                pe.wait_ge(t["x_ready"], c + 1)
                if later(c, 1):
                    pe.wait_ge(t["s_ready"], c)
                for j in tiles:
                    last = pe.transpose(tile(t["ps_s"], j), tile(xs[k], j), w["ident"][:, :])
                last.then_inc(t["transposed"], 1)

            run_slots(pe, EDGE_CHUNKS, first, [(3, project), (2, x_to_cols)])


def node_layer(nc, w, name, x_tab, neigh, out_tab, deep):
    with ExitStack() as ctx:
        t = {"phase": name}
        alloc(nc, ctx, t, "cn0 cn1 xn0 xn1 hT0 hT1 h10 h11 h20 h21 new0 new1", [P, CHUNK])
        alloc(nc, ctx, t, "x_ring", [P, RING * CHUNK])
        alloc(nc, ctx, t, "st", [P, 6 * TILES])
        alloc(nc, ctx, t, "mom0 mom1", [P, 2 * TILES])
        alloc(nc, ctx, t, "lv rs0 rs1", [P, TILES])
        alloc(nc, ctx, t, "ps_s ps_o ps_1 ps_2", [P, CHUNK], F32, "psum")
        semaphores(nc, ctx, t, "x_in0 x_in1 n_in0 n_in1 out0 out1 stats rstd x_ready transposed h_ready "
                               "first_done h1_ready second_done h2_ready out_done new_ready")
        two = lambda name: (t[name + "0"], t[name + "1"])
        cn, xn, hT, h1, h2, new, mom, rs = (two(n) for n in "cn xn hT h1 h2 new mom rs".split())
        x_in, n_in, s_out = (two(n) for n in "x_in n_in out".split())
        last_lag = 6 if deep else 4
        first = 8
        tiles = range(TILES)
        block = ctx.enter_context(nc.Block())

        def ring(c, j=0, width=D):
            return t["x_ring"][:, bass.ds((c & (RING - 1)) * CHUNK + j * D, width)]

        @block.sync
        def _(sp):
            def earlier_x(c, k):
                if later(c, 2):
                    sp.wait_ge(x_in[k], (c - k) * (DMA // 2))

            def load_x(c, k):
                sp.dma_start(ring(c, 0, CHUNK), nodes(x_tab, c)).then_inc(x_in[k], DMA)

            def neigh_free(c, k):
                if later(c, 2):
                    wait_apart(sp, t["first_done" if deep else "out_done"], c - 1)

            def load_neigh(c, k):
                sp.dma_start(cn[k][:, :], nodes(neigh, c)).then_inc(n_in[k], DMA)

            def store(c, k):
                wait_apart(sp, t["new_ready"], c + 1)
                sp.dma_start(nodes(out_tab, c), new[k][:, :]).then_inc(s_out[k], DMA)

            run_slots(sp, NODE_CHUNKS, first, [(last_lag + 1, store), (3, neigh_free), (0, earlier_x),
                                               (3, load_neigh), (0, load_x)])
            for k in range(2):
                sp.wait_ge(s_out[k], DMA * (NODE_CHUNKS // 2))

        @block.vector
        def _(v):
            v.sem_inc(t["transposed"], 2)

            def stats(c, k):
                v.wait_ge(x_in[k], (c - k) * (DMA // 2) + DMA)
                row_stats(v, [ring(c, j) for j in tiles], t["st"], mom[k]).then_inc(t["stats"], 1)

            def norm(c, k):
                v.wait_ge(t["rstd"], c + 1)
                v.wait_ge(t["transposed"], c + 1)
                normalise(v, [tile(xn[k], j) for j in tiles], [ring(c, j) for j in tiles],
                          mom[k], rs[k]).then_inc(t["x_ready"], 1)

            def new_rows(c, k):
                v.wait_ge(t["out_done"], c + 1)
                if later(c, 2):
                    v.wait_ge(s_out[k], (c - k) * (DMA // 2))
                v.tensor_tensor(new[k][:, :], t["ps_o"][:, :], ring(c, 0, CHUNK), ALU.add).then_inc(t["new_ready"], 1)

            run_slots(v, NODE_CHUNKS, first, [(3, norm), (2, stats), (last_lag, new_rows)])

        @block.scalar
        def _(a):
            def rstd(c, k):
                a.wait_ge(t["stats"], c + 1)
                inverse_std(a, mom[k], t["lv"], rs[k], TILES, w["eps_col"][:, 0:1]).then_inc(t["rstd"], 1)

            def to_sbuf(c, k):
                a.wait_ge(t["transposed"], c + 3)
                a.activation(hT[k][:, :], t["ps_s"][:, :], ACT.Relu).then_inc(t["h_ready"], 1)

            def first_relu(c, k):
                a.wait_ge(t["first_done"], c + 1)
                a.activation(h1[k][:, :], t["ps_1"][:, :], ACT.Relu, bias=w["l3_bself"][:, 0:1]).then_inc(t["h1_ready"], 1)

            def second_relu(c, k):
                a.wait_ge(t["second_done"], c + 1)
                a.activation(h2[k][:, :], t["ps_2"][:, :], ACT.Relu, bias=w["l3_bfc1"][:, 0:1]).then_inc(t["h2_ready"], 1)

            more = [(5, second_relu), (4, first_relu)] if deep else []
            run_slots(a, NODE_CHUNKS, first, [(0, log_exp_tables(a))] + more + [(3, to_sbuf), (2, rstd)])

        @block.tensor
        def _(pe):
            def x_to_cols(c, k):
                pe.wait_ge(t["x_ready"], c + 1)
                if later(c, 1):
                    pe.wait_ge(t["h_ready"], c)
                for j in tiles:
                    last = pe.transpose(tile(t["ps_s"], j), tile(xn[k], j), w["ident"][:, :])
                last.then_inc(t["transposed"], 1)

            def layer_2(c, k):
                pe.wait_ge(t["h_ready"], c + 1)
                pe.wait_ge(n_in[k], (c - k) * (DMA // 2) + DMA)
                if later(c, 1):
                    pe.wait_ge(t["new_ready"], c)
                pe.matmul(t["ps_o"][:, :], w["ones_row"][:, :], w["l2_b4"][:, :], start=True, stop=False)
                for j in tiles:
                    pe.matmul(tile(t["ps_o"], j), tile(hT[k], j), w["l2_wT"][:, :], start=False, stop=False)
                pe.matmul(t["ps_o"][:, :], w["ident"][:, :], cn[k][:, :], start=False, stop=True).then_inc(t["out_done"], 1)

            def self_and_neigh(c, k):
                pe.wait_ge(t["h_ready"], c + 1)
                pe.wait_ge(n_in[k], (c - k) * (DMA // 2) + DMA)
                if later(c, 1):
                    pe.wait_ge(t["h1_ready"], c)
                pe.matmul(t["ps_1"][:, :], w["l3_self"][:, :], hT[k][:, :], start=True, stop=False)
                for j in tiles:
                    last = pe.matmul(tile(t["ps_1"], j), tile(cn[k], j), w["ident"][:, :], start=False, stop=j == TILES - 1)
                last.then_inc(t["first_done"], 1)

            def fc1(c, k):
                pe.wait_ge(t["h1_ready"], c + 1)
                if later(c, 1):
                    pe.wait_ge(t["h2_ready"], c)
                pe.matmul(t["ps_2"][:, :], w["l3_fc1"][:, :], h1[k][:, :], start=True, stop=True).then_inc(t["second_done"], 1)

            def fc2(c, k):
                pe.wait_ge(t["h2_ready"], c + 1)
                if later(c, 1):
                    pe.wait_ge(t["new_ready"], c)
                pe.matmul(t["ps_o"][:, :], w["ones_row"][:, :], w["l3_b4"][:, :], start=True, stop=False)
                for j in tiles:
                    last = pe.matmul(tile(t["ps_o"], j), tile(h2[k], j), w["l3_fc2"][:, :], start=False, stop=j == TILES - 1)
                last.then_inc(t["out_done"], 1)

            after = [(6, fc2), (5, fc1), (4, self_and_neigh)] if deep else [(4, layer_2)]
            run_slots(pe, NODE_CHUNKS, first, after + [(3, x_to_cols)])


def bass_four_graph_layers(nc, inp, out):
    with ExitStack() as ctx:
        w = {"phase": "all"}
        alloc(nc, ctx, w, "wqkv", [P, 3 * D])
        alloc(nc, ctx, w, "w1", [P, HIDDEN])
        alloc(nc, ctx, w, "w2", [P, HC * D])
        alloc(nc, ctx, w, "bqkv", [P, 3])
        alloc(nc, ctx, w, "bk_scaled l3_bself l3_bfc1 eps_col", [P, 1])
        alloc(nc, ctx, w, "b1", [P, HC])
        alloc(nc, ctx, w, "norm_w norm_b ident l1_w l1_wsrc l1_wdst l2_wT l3_neigh l3_self l3_fc1 l3_fc2", [P, D])
        alloc(nc, ctx, w, "lc4 c4 l1_b4 ones_wide", [P, CHUNK])
        alloc(nc, ctx, w, "l2_b4 l3_b4", [1, CHUNK])
        alloc(nc, ctx, w, "ones_row neg_row c_row", [1, D])
        alloc(nc, ctx, w, "src_idx dst_idx end_idx", [P, EDGE_CHUNKS * TILES], I32)
        alloc(nc, ctx, w, "rdeg", [P, EDGE_CHUNKS * TILES])
        alloc(nc, ctx, w, "run_gap", [P, EP], BF16)
        dram = lambda name, rows: nc.dram_tensor(name, [rows, D], F32).ap()
        tables, x1_tab, x2_tab, x3_tab, neigh = (dram(n, r) for n, r in (
            ("h_tables", 2 * NP), ("x1_table", NP), ("x2_table", NP), ("x3_table", NP), ("neighbours", NP)))
        setup(nc, w, inp)
        start_tables(nc, w, inp, tables, neigh)
        attention_rounds(nc, w, tables)
        close_rounds(nc, w, inp, tables, x1_tab, x2_tab)
        graph_attention(nc, w, x1_tab, x2_tab)
        average_neighbours(nc, w, "mean2", x2_tab, w["l2_wT"], neigh)
        node_layer(nc, w, "nodes2", x2_tab, neigh, x3_tab, deep=False)
        average_neighbours(nc, w, "mean3", x3_tab, w["l3_neigh"], neigh)
        node_layer(nc, w, "nodes3", x3_tab, neigh, out, deep=True)


_NAMES = ['L0_gnn_norm_w', 'L0_gnn_norm_b', 'L0_gnn_nin_w', 'L0_gnn_nin_b', 'L0_gnn_Wqkv', 'L0_gnn_no_w',
          'L0_gnn_no_b', 'L0_gnn_W1', 'L0_gnn_b1', 'L0_gnn_W2', 'L0_gnn_b2', 'L1_gnn_W', 'L1_gnn_att',
          'L1_gnn_bias', 'L2_gnn_W', 'L2_gnn_b', 'L3_gnn_W_neigh', 'L3_gnn_W_self', 'L3_gnn_b_self',
          'L3_gnn_W_fc1', 'L3_gnn_b_fc1', 'L3_gnn_W_fc2', 'L3_gnn_b_fc2']


def kernel(**inputs):
    import numpy as np
    import concourse.bacc as bacc
    from concourse.bass_utils import run_bass_kernel_spmd

    nc = bacc.Bacc("TRN2", target_bir_lowering=False, num_devices=1)
    arrays = {n: np.ascontiguousarray(inputs[n]) for n in _NAMES}
    x = np.asarray(inputs["x"])
    arrays["x"] = np.concatenate([x, np.zeros((NP - N, D), x.dtype)])
    src, dst = np.asarray(inputs["src"]), np.asarray(inputs["dst"])
    pad = lambda a, fill, n: np.concatenate([a, np.full(n, fill, a.dtype)])
    tiles = lambda a: np.ascontiguousarray(a.reshape(EP // P, P).T)
    ext = pad(dst, N, EP + 1 - E)
    arrays["src_t"] = tiles(pad(src, 0, EP - E))
    arrays["dst_t"] = tiles(ext[:EP])
    arrays["dst_next_t"] = tiles(ext[1:EP + 1])
    arrays["dst_ext"] = np.concatenate([np.full(1, -1, dst.dtype), ext[:EP]])
    inp = {n: nc.dram_tensor(f"in_{n}", a.shape, mybir.dt.from_np(a.dtype), kind="ExternalInput").ap()
           for n, a in arrays.items()}
    out = nc.dram_tensor("out_0", (NP, D), F32, kind="ExternalOutput").ap()
    bass_four_graph_layers(nc, inp, out)
    r = run_bass_kernel_spmd(nc, [{f"in_{n}": a for n, a in arrays.items()}], core_ids=[0])
    return r.results[0]["out_0"][:N]
```

```python
from contextlib import ExitStack

import concourse.bass as bass
from concourse import mybir

F32 = mybir.dt.float32
I32 = mybir.dt.int32
BF16 = mybir.dt.bfloat16
ALU = mybir.AluOpType
ACT = mybir.ActivationFunctionType
AX = bass.IndirectOffsetOnAxis

P = 128
D = 128
N = 50000
E = 25000
TILES = 4
CHUNK = TILES * P
EDGE_CHUNKS = 50
NODE_CHUNKS = 98
NP = NODE_CHUNKS * CHUNK
EP = EDGE_CHUNKS * CHUNK
UNIT = 2 * CHUNK
UNITS = NP // UNIT
MARKS = 5 * CHUNK
HIDDEN = 4 * D
HC = HIDDEN // P
ROUNDS = 3
HEADS = 4
HEAD = D // HEADS
EPS = 1e-5
GAP = -(2.0 ** 100)
SKIP = 1 << 20
QK_SCALE = float(D) ** -0.5
RING = 8
DMA = 16


def run_slots(eng, n, first, stages):
    deepest = max(lag for lag, _ in stages if lag is not None)
    assert deepest <= first and (n - first) % 2 == 0

    def slot(s):
        for lag, body in stages:
            if lag is None:
                body()
            elif 0 <= s - lag < n:
                body(s - lag, (s - lag) % 2)

    for s in range(first):
        slot(s)
    with eng.Fori(0, (n - first) // 2) as i:
        twice = eng.snap(2 * i)
        for k in range(2):
            for lag, body in stages:
                if lag is None:
                    body()
                else:
                    body(twice + (first + k - lag), (first + k - lag) % 2)
    for s in range(n, n + deepest):
        slot(s)


def later(c, n):
    return not isinstance(c, int) or c >= n


def tile(ap, j, width=D):
    return ap[:, j * width:(j + 1) * width]


def alloc(nc, ctx, made, names, shape, dt=F32, space="sbuf"):
    make = nc.sbuf_tensor if space == "sbuf" else nc.psum_tensor
    for name in names.split():
        made[name] = ctx.enter_context(make(f"{made['phase']}_{name}", shape, dt))


def semaphores(nc, ctx, made, names):
    for name in names.split():
        made[name] = ctx.enter_context(nc.semaphore(f"{made['phase']}_{name}"))


def wait_apart(eng, sem, value):
    if not isinstance(value, int):
        eng.wait_ge(sem, 1)
    eng.wait_ge(sem, value)


def partial_stats(v, rows, stats):
    for j, r in enumerate(rows):
        v.bn_stats(stats[:, 6 * j:6 * j + 6], r)


def moments_of(v, stats, moments, n):
    for j in range(n):
        last = v.bn_aggr(moments[:, 2 * j:2 * j + 2], stats[:, 6 * j:6 * j + 6])
    return last


def row_stats(v, rows, stats, moments):
    partial_stats(v, rows, stats)
    v.drain()
    return moments_of(v, stats, moments, len(rows))


def inverse_std(a, moments, log_var, rstd, n, eps_col):
    var = moments[:, 0:2 * n].rearrange("p (n two) -> p n two", two=2)[:, :, 1]
    a.activation(log_var[:, 0:n], var, ACT.Ln, bias=eps_col)
    a.drain()
    return a.activation(rstd[:, 0:n], log_var[:, 0:n], ACT.Exp, scale=-0.5)


def shift_of(v, shift, moments, rstd, n):
    mean = moments[:, 0:2 * n].rearrange("p (n two) -> p n two", two=2)[:, :, 0]
    return v.scalar_tensor_tensor(shift[:, 0:n], mean, -1.0, rstd[:, 0:n], ALU.mult, ALU.mult)


def scale_and_shift(a, outs, rows, rstd, shift):
    for j, (o, r) in enumerate(zip(outs, rows)):
        last = a.activation(o, r, ACT.Identity, bias=shift[:, j:j + 1], scale=rstd[:, j:j + 1])
    return last


def log_exp_tables(a):
    return lambda c, k: a.preload_act_table_set("natural_log_exp_and_others") if k == 0 else None


def normalise(v, outs, rows, moments, rstd, at=0):
    for j, (o, r) in enumerate(zip(outs, rows)):
        k = at + j
        last = v.tensor_scalar(o, r, moments[:, 2 * k:2 * k + 1], rstd[:, k:k + 1],
                               ALU.subtract, ALU.mult)
    return last


def setup(nc, w, inp):
    with ExitStack() as ctx:
        t = {"phase": "setup"}
        alloc(nc, ctx, t, "wqkv_raw", [P, 3 * D])
        alloc(nc, ctx, t, "w1_raw", [P, HIDDEN])
        alloc(nc, ctx, t, "nin_w nin_b no_w no_b asrc adst", [P, 1])
        alloc(nc, ctx, t, "b1_raw gelu_b1", [P, HC])
        alloc(nc, ctx, t, "w2l2_raw l1_wT block_src block_dst", [P, D])
        alloc(nc, ctx, t, "b2_row c0_row l1b_row", [1, D])
        alloc(nc, ctx, t, "c_row4", [1, CHUNK])
        alloc(nc, ctx, t, "dst_next", [P, EDGE_CHUNKS * TILES], I32)
        alloc(nc, ctx, t, "not_last", [P, EDGE_CHUNKS * TILES])
        alloc(nc, ctx, t, "dst0 dst1", [P, 1 + MARKS], I32)
        alloc(nc, ctx, t, "same ones", [P, MARKS])
        alloc(nc, ctx, t, "count0 count1", [P, MARKS])
        alloc(nc, ctx, t, "ps_row", [1, CHUNK], F32, "psum")
        alloc(nc, ctx, t, "ps_a ps_b ps_c ps_d ps_cnt0 ps_cnt1", [P, CHUNK], F32, "psum")
        semaphores(nc, ctx, t,
                   "loaded dst_sem0 dst_sem1 zeroed ident_ready blocks pe_out dve_out act_out "
                   "counted count_cols count_used")
        dst = (t["dst0"], t["dst1"])
        steps = EP // MARKS
        count, ps_cnt, dst_sem = (t["count0"], t["count1"]), (t["ps_cnt0"], t["ps_cnt1"]), (t["dst_sem0"], t["dst_sem1"])
        col = lambda x: x.rearrange("(p a) -> p a", a=1)
        row = lambda x: x.rearrange("(a n) -> a n", a=1)
        loads = [
            (t["wqkv_raw"][:, :], inp["L0_gnn_Wqkv"][:, :]),
            (t["w1_raw"][:, :], inp["L0_gnn_W1"][:, :]),
            (w["w2"][:, :].rearrange("p (j n) -> p j n", j=HC),
             inp["L0_gnn_W2"].rearrange("(j p) n -> p j n", p=P)),
            (t["nin_w"][:, :], col(inp["L0_gnn_nin_w"])), (t["nin_b"][:, :], col(inp["L0_gnn_nin_b"])),
            (t["no_w"][:, :], col(inp["L0_gnn_no_w"])), (t["no_b"][:, :], col(inp["L0_gnn_no_b"])),
            (t["b2_row"][:, :], row(inp["L0_gnn_b2"])),
            (w["norm_w"][:, :], inp["L0_gnn_norm_w"].partition_broadcast(P)),
            (w["norm_b"][:, :], inp["L0_gnn_norm_b"].partition_broadcast(P)),
            (w["l1_w"][:, :], inp["L1_gnn_W"][:, :]),
            (t["l1b_row"][:, :], row(inp["L1_gnn_bias"])),
            (t["w2l2_raw"][:, :], inp["L2_gnn_W"][:, :]),
            (w["l3_neigh"][:, :], inp["L3_gnn_W_neigh"][:, :]),
            (w["l3_self"][:, :], inp["L3_gnn_W_self"][:, :]),
            (w["l3_fc1"][:, :], inp["L3_gnn_W_fc1"][:, :]),
            (w["l3_fc2"][:, :], inp["L3_gnn_W_fc2"][:, :]),
            (w["l3_bself"][:, :], col(inp["L3_gnn_b_self"])),
            (w["l3_bfc1"][:, :], col(inp["L3_gnn_b_fc1"])),
            (w["src_idx"][:, :], inp["src_t"][:, :]), (w["dst_idx"][:, :], inp["dst_t"][:, :]),
            (t["dst_next"][:, :], inp["dst_next_t"][:, :]),
        ]
        for j in range(HC):
            loads.append((t["b1_raw"][:, j:j + 1], col(inp["L0_gnn_b1"][j * P:(j + 1) * P])))
        for h in range(HEADS):
            loads.append((t["asrc"][h * HEAD:(h + 1) * HEAD, :], col(inp["L1_gnn_att"][h, 0:HEAD])))
            loads.append((t["adst"][h * HEAD:(h + 1) * HEAD, :], col(inp["L1_gnn_att"][h, HEAD:2 * HEAD])))
        for j in range(TILES):
            loads.append((tile(w["l2_b4"], j), row(inp["L2_gnn_b"])))
            loads.append((tile(w["l3_b4"], j), inp["L3_gnn_b_fc2"].partition_broadcast(P)))
        block = ctx.enter_context(nc.Block())

        @block.sync
        def _(sp):
            for to, frm in loads:
                sp.dma_start(to, frm).then_inc(t["loaded"], DMA)
            def load(c, k):
                sp.dma_start(dst[k][:, :], inp["dst_ext"][bass.ds(c * MARKS, 1 + MARKS)].partition_broadcast(P))\
                  .then_inc(dst_sem[k], DMA)

            for k in range(2):
                load(k, k)
            with sp.Fori(0, steps // 2 - 1) as i:
                for k in range(2):
                    wait_apart(sp, t["counted"], 2 * i + (k + 1))
                    load(2 * i + (2 + k), k)

        @block.gpsimd
        def _(pool):
            pool.memset(w["ident"][:, :], 0.0).then_inc(t["zeroed"], 1)
            pool.memset(w["ones_row"][:, :], 1.0)
            pool.memset(w["eps_col"][:, :], EPS)
            pool.wait_ge(t["zeroed"], 1)
            pool.affine_select(out=w["ident"][:, :], in_=w["ident"][:, :], compare_op=ALU.not_equal, fill=1.0,
                               base=0, pattern=[[-1, P]], channel_multiplier=1).then_inc(t["ident_ready"], 1)

        @block.vector
        def _(v):
            v.memset(t["block_src"][:, :], 0.0)
            v.memset(t["block_dst"][:, :], 0.0)
            v.drain()
            for h in range(HEADS):
                for m in (t["block_src"], t["block_dst"]):
                    v.memset(m[h * HEAD:(h + 1) * HEAD, h * HEAD:(h + 1) * HEAD], 1.0)
            v.wait_ge(t["loaded"], DMA * len(loads))
            v.tensor_scalar(w["wqkv"][:, :], t["wqkv_raw"][:, :], t["nin_w"][:, 0:1], None, ALU.mult)
            v.tensor_scalar(w["w1"][:, :], t["w1_raw"][:, :], t["no_w"][:, 0:1], None, ALU.mult)
            v.drain()
            v.tensor_scalar(t["block_src"][:, :], t["block_src"][:, :], t["asrc"][:, 0:1], None, ALU.mult)
            v.tensor_scalar(t["block_dst"][:, :], t["block_dst"][:, :], t["adst"][:, 0:1], None, ALU.mult)\
             .then_inc(t["blocks"], 1)
            v.tensor_tensor(t["not_last"][:, :], w["dst_idx"][:, :], t["dst_next"][:, :], ALU.is_equal)
            v.drain()
            v.scalar_tensor_tensor(w["end_idx"][:, :], t["not_last"][:, :], float(SKIP), w["dst_idx"][:, :],
                                   ALU.mult, ALU.add)
            v.memset(w["lc4"][:, :], 0.0)
            v.wait_ge(t["pe_out"], 1)
            v.tensor_copy(w["bqkv"][:, :], t["ps_a"][:, 0:3])
            v.tensor_tensor(w["b1"][:, :], t["ps_a"][:, 4:4 + HC], t["b1_raw"][:, :], ALU.add)
            v.tensor_copy(w["l2_wT"][:, :], t["ps_b"][:, 0:D])
            v.tensor_copy(t["l1_wT"][:, :], t["ps_b"][:, D:2 * D])
            v.drain()
            v.tensor_scalar(w["bk_scaled"][:, :], w["bqkv"][:, 1:2], QK_SCALE, None, ALU.mult).then_inc(t["dve_out"], 1)
            v.wait_ge(t["pe_out"], 2)
            v.tensor_copy(w["l1_wsrc"][:, :], t["ps_c"][:, 0:D])
            v.tensor_copy(w["l1_wdst"][:, :], t["ps_c"][:, D:2 * D])
            v.tensor_copy(t["c0_row"][:, :], t["ps_row"][:, 0:D])
            v.drain()
            v.tensor_scalar(w["neg_row"][:, :], t["c0_row"][:, :], -1.0, None, ALU.mult)
            v.tensor_tensor(w["c_row"][:, :], t["c0_row"][:, :], t["b2_row"][:, :], ALU.add)
            v.drain()
            for j in range(TILES):
                v.tensor_copy(tile(t["c_row4"], j), w["c_row"][:, :])
            v.drain().then_inc(t["dve_out"], 1)
            v.wait_ge(t["pe_out"], 3)
            v.tensor_copy(w["c4"][:, :], t["ps_a"][:, :])
            for j in range(TILES):
                v.tensor_copy(tile(w["l1_b4"], j), t["ps_b"][:, 0:D])
            v.memset(count[1][:, MARKS - 1:MARKS], 0.0)
            v.drain()

            def marks(c, k):
                v.wait_ge(dst_sem[k], (c - k) * (DMA // 2) + DMA)
                v.tensor_tensor(t["same"][:, :], dst[k][:, 1:1 + MARKS], dst[k][:, 0:MARKS], ALU.is_equal)
                v.drain()
                v.tensor_scalar(w["run_gap"][:, bass.ds(c * MARKS, MARKS)], t["same"][:, :], 1.0, -GAP,
                                ALU.subtract, ALU.mult)
                v.tensor_tensor_scan(count[k][:, :], t["same"][:, :], t["ones"][:, :],
                                     count[1 - k][:, MARKS - 1:MARKS], ALU.mult, ALU.add)\
                 .then_inc(t["counted"], 1)
                v.drain()

            def degrees(c, k):
                v.wait_ge(t["count_cols"], c + 1)
                v.tensor_scalar(w["rdeg"][:, bass.ds(c * (MARKS // P), MARKS // P)], ps_cnt[k][:, 0:MARKS // P],
                                1.0, None, ALU.max)

            v.memset(t["ones"][:, :], 1.0)
            v.drain()
            run_slots(v, steps, 2, [(0, marks), (1, degrees)])
            v.drain()
            v.reciprocal(w["rdeg"][:, :], w["rdeg"][:, :])

        @block.scalar
        def _(a):
            a.wait_ge(t["dve_out"], 1)
            a.activation(t["gelu_b1"][:, :], w["b1"][:, :], ACT.Gelu).then_inc(t["act_out"], 1)

        @block.tensor
        def _(pe):
            pe.wait_ge(t["loaded"], DMA * len(loads))
            pe.wait_ge(t["ident_ready"], 1)
            for j in range(3):
                pe.matmul(t["ps_a"][:, j:j + 1], tile(t["wqkv_raw"], j), t["nin_b"][:, 0:1], start=True, stop=True)
            for j in range(HC):
                pe.matmul(t["ps_a"][:, 4 + j:5 + j], tile(t["w1_raw"], j), t["no_b"][:, 0:1], start=True, stop=True)
            pe.transpose(t["ps_b"][:, 0:D], t["w2l2_raw"][:, :], w["ident"][:, :])
            pe.transpose(t["ps_b"][:, D:2 * D], w["l1_w"][:, :], w["ident"][:, :]).then_inc(t["pe_out"], 1)
            pe.wait_ge(t["dve_out"], 1)
            pe.wait_ge(t["blocks"], 1)
            pe.matmul(t["ps_c"][:, 0:D], t["l1_wT"][:, :], t["block_src"][:, :], start=True, stop=True)
            pe.matmul(t["ps_c"][:, D:2 * D], t["l1_wT"][:, :], t["block_dst"][:, :], start=True, stop=True)
            pe.wait_ge(t["act_out"], 1)
            for j in range(HC):
                last = pe.matmul(t["ps_row"][:, 0:D], t["gelu_b1"][:, j:j + 1], tile(w["w2"], j),
                                 start=j == 0, stop=j == HC - 1)
            last.then_inc(t["pe_out"], 1)
            pe.wait_ge(t["dve_out"], 2)
            pe.matmul(t["ps_a"][:, :], w["ones_row"][:, :], t["c_row4"][:, :], start=True, stop=True)
            pe.matmul(t["ps_b"][:, 0:D], w["ones_row"][:, :], t["l1b_row"][:, :], start=True, stop=True)\
              .then_inc(t["pe_out"], 1)

            def count_columns(c, k):
                pe.wait_ge(t["counted"], c + 1)
                for j in range(MARKS // P):
                    last = pe.matmul(ps_cnt[k][:, j:j + 1], tile(count[k], j)[0:1, :],
                                     w["ones_row"][0:1, 0:1], start=True, stop=True)
                last.then_inc(t["count_cols"], 1)

            run_slots(pe, steps, 2, [(0, count_columns)])


def nodes(tab, c, at=0):
    return tab[bass.ds(c * CHUNK + at, CHUNK), :].rearrange("(p j) d -> p (j d)", p=P)


def unit(tab, c, at=0):
    return tab[bass.ds(c * UNIT + at, UNIT), :].rearrange("(p j) d -> p (j d)", p=P)


def start_tables(nc, w, inp, tables):
    with ExitStack() as ctx:
        t = {"phase": "start"}
        alloc(nc, ctx, t, "y0 y1", [P, CHUNK])
        alloc(nc, ctx, t, "x_ring", [P, RING * CHUNK])
        alloc(nc, ctx, t, "st0 st1", [P, 6 * TILES])
        alloc(nc, ctx, t, "mom0 mom1", [P, 2 * TILES])
        alloc(nc, ctx, t, "lv0 lv1 rs0 rs1", [P, TILES])
        semaphores(nc, ctx, t, "in0 in1 out0 out1 stats_done rstd_done norm_done relu_done")
        two = lambda name: (t[name + "0"], t[name + "1"])
        y, st, mom, lv, rs, s_in, s_out = (two(n) for n in "y st mom lv rs in out".split())
        first = 4
        tiles = range(TILES)
        ring = lambda c, j=0, width=D: t["x_ring"][:, bass.ds((c & (RING - 1)) * CHUNK + j * D, width)]
        block = ctx.enter_context(nc.Block())

        @block.sync
        def _(sp):
            def earlier_load(c, k):
                if later(c, 2):
                    sp.wait_ge(s_in[k], (c - k) * (DMA // 2))

            def load(c, k):
                sp.dma_start(ring(c, 0, CHUNK), nodes(inp["x"], c)).then_inc(s_in[k], DMA)

            def store(c, k):
                wait_apart(sp, t["relu_done"], c + 1)
                sp.dma_start(nodes(tables, c), y[k][:, :]).then_inc(s_out[k], DMA)

            def store_again(c, k):
                sp.dma_start(nodes(tables, c, NP), y[k][:, :]).then_inc(s_out[k], DMA)

            run_slots(sp, NODE_CHUNKS, first, [(4, store), (0, earlier_load), (4, store_again), (0, load)])
            for k in range(2):
                sp.wait_ge(s_out[k], 2 * DMA * (NODE_CHUNKS // 2))

        @block.vector
        def _(v):
            def stats(c, k):
                v.wait_ge(s_in[k], (c - k) * (DMA // 2) + DMA)
                row_stats(v, [ring(c, j) for j in tiles], st[k], mom[k]).then_inc(t["stats_done"], 1)

            def norm(c, k):
                v.wait_ge(t["rstd_done"], c + 1)
                if later(c, 2):
                    v.wait_ge(s_out[k], (c - k) * DMA)
                normalise(v, [tile(y[k], j) for j in tiles], [ring(c, j) for j in tiles],
                          mom[k], rs[k]).then_inc(t["norm_done"], 1)

            run_slots(v, NODE_CHUNKS, first, [(2, stats), (3, norm)])

        @block.scalar
        def _(a):
            def rstd(c, k):
                a.wait_ge(t["stats_done"], c + 1)
                inverse_std(a, mom[k], lv[k], rs[k], TILES, w["eps_col"][:, 0:1]).then_inc(t["rstd_done"], 1)

            def relu(c, k):
                a.wait_ge(t["norm_done"], c + 1)
                a.activation(y[k][:, :], y[k][:, :], ACT.Relu).then_inc(t["relu_done"], 1)

            run_slots(a, NODE_CHUNKS, first, [(0, log_exp_tables(a)), (2, rstd), (3, relu)])


def attention_rounds(nc, w, tables):
    with ExitStack() as ctx:
        t = {"phase": "rounds"}
        alloc(nc, ctx, t, "gs0 gs1 gd0 gd1 hs0 hs1 xs0 xs1 xd0 xd1 sT0 sT1 dT0 dT1 ks0 ks1 att0 att1 "
                          "z0 z1 u0 u1 r0 r1 ve n30 n31 nT0 nT1 lz rz0 rz1 new0 new1", [P, CHUNK])
        alloc(nc, ctx, t, "hd_ring", [P, RING * CHUNK])
        alloc(nc, ctx, t, "m0 m1", [P, 1 + CHUNK])
        alloc(nc, ctx, t, "d0 d1", [P, 2 * CHUNK])
        alloc(nc, ctx, t, "hid0 hid1", [P, HC * CHUNK])
        alloc(nc, ctx, t, "st1 st2 st3", [P, 12 * TILES])
        alloc(nc, ctx, t, "ma0 ma1 mb0 mb1 mc0 mc1", [P, 4 * TILES])
        alloc(nc, ctx, t, "lv1 lv2 lv3 ra0 ra1 rb0 rb1 rc0 rc1 nb0 nb1 nc0 nc1", [P, 2 * TILES])
        alloc(nc, ctx, t, "idx_read0 idx_read1", [P, 2 * TILES], I32)
        alloc(nc, ctx, t, "idx_end0 idx_end1 read_half write_half half_step", [P, TILES], I32)
        alloc(nc, ctx, t, "ps_s ps_d ps_q ps_k ps_v ps_r ps_hid ps_y", [P, CHUNK], F32, "psum")
        semaphores(nc, ctx, t,
                   "halves idx_made end_made gathered0 gathered1 rows_in stats1 rstd1 stats2 rstd2 shift2 "
                   "x_ready transposed sd_ready k_done qv_done k_ready arg_ready exp_done v_used "
                   "zu_ready rz_ready r_ready r_rows stats3 rstd3 shift3 n3_ready n3_cols nT_ready hid_done "
                   "gelu_done y_done new_ready scattered0 scattered1 round_set")
        two = lambda name: (t[name + "0"], t[name + "1"])
        gs, gd, hs, xs, xd, sT, dT, ks, att = (two(n) for n in "gs gd hs xs xd sT dT ks att".split())
        z, u, r, n3, nT, rz, new, m, d, hid = (two(n) for n in "z u r n3 nT rz new m d hid".split())
        ma, mb, mc, ra, rb, rc = (two(n) for n in "ma mb mc ra rb rc".split())
        shift2, shift3 = (two(n) for n in "nb nc".split())
        idx_read, idx_end, gathered, scattered = (two(n) for n in "idx_read idx_end gathered scattered".split())
        first = 10
        tiles = range(TILES)
        hid_bank = (t["ps_hid"], t["ps_d"])

        def chunks_before_up(base, c):
            return base + (min(c + 3, EDGE_CHUNKS) if isinstance(c, int) else c + 3)

        def ring(g, j=0, width=D):
            return t["hd_ring"][:, bass.ds((g & (RING - 1)) * CHUNK + j * D, width)]

        block = ctx.enter_context(nc.Block())

        @block.gpsimd
        def _(pool):
            pool.sem_inc(t["rows_in"], 2)
            pool.memset(t["read_half"][:, :], 0)
            pool.memset(t["write_half"][:, :], NP)
            pool.memset(t["half_step"][:, :], NP).then_inc(t["halves"], 1)
            pool.wait_ge(t["halves"], 1)
            with pool.Fori(0, ROUNDS) as rnd:
                base = pool.snap(rnd * EDGE_CHUNKS)
                wait_apart(pool, t["round_set"], rnd + 1)

                def gather(c, k):
                    g = base + c
                    pool.wait_ge(t["rows_in"], g + 1)
                    cols = bass.ds(c * TILES, TILES)
                    pool.tensor_tensor(idx_read[k][:, 0:TILES], w["src_idx"][:, cols], t["read_half"][:, :], ALU.add)
                    pool.tensor_tensor(idx_read[k][:, TILES:2 * TILES], w["dst_idx"][:, cols], t["read_half"][:, :],
                                       ALU.add).then_inc(t["idx_made"], 1)
                    wait_apart(pool, t["idx_made"], g + 1)
                    for rows, at in ((gs[k], 0), (gd[k], TILES)):
                        for j in tiles:
                            pool.indirect_dma_start(
                                out=tile(rows, j), out_offset=None, in_=tables[:, :],
                                in_offset=AX(ap=idx_read[k][:, at + j:at + j + 1], axis=0))\
                                .then_inc(gathered[k], DMA)

                def add_lc(c, k):
                    g = base + c
                    if later(c, 2):
                        pool.wait_ge(t["stats2"], g - 1)
                    pool.wait_ge(gathered[k], (g - k) * (DMA * TILES) + 2 * TILES * DMA)
                    pool.tensor_tensor(hs[k][:, :], gs[k][:, :], w["lc4"][:, :], ALU.add)
                    pool.tensor_tensor(ring(g, 0, CHUNK), gd[k][:, :], w["lc4"][:, :], ALU.add).then_inc(t["rows_in"], 1)

                def scatter(c, k):
                    g = base + c
                    pool.wait_ge(t["new_ready"], g + 1)
                    if later(c, 2):
                        pool.wait_ge(scattered[k], (g - k) * (DMA * TILES // 2))
                    pool.tensor_tensor(idx_end[k][:, :], w["end_idx"][:, bass.ds(c * TILES, TILES)],
                                       t["write_half"][:, :], ALU.add).then_inc(t["end_made"], 1)
                    wait_apart(pool, t["end_made"], g + 1)
                    for j in tiles:
                        pool.indirect_dma_start(
                            out=tables[:, :], out_offset=AX(ap=idx_end[k][:, j:j + 1], axis=0),
                            in_=tile(new[k], j), in_offset=None, bounds_check=2 * NP - 1,
                            oob_is_err=False).then_inc(scattered[k], DMA)

                run_slots(pool, EDGE_CHUNKS, first, [
                    (10, scatter), (2, add_lc), (0, gather)])
                for k in range(2):
                    pool.wait_ge(scattered[k], (base + EDGE_CHUNKS) * (DMA * TILES // 2))
                for half in (t["read_half"], t["write_half"]):
                    last = pool.tensor_tensor(half[:, :], t["half_step"][:, :], half[:, :], ALU.subtract)
                last.then_inc(t["halves"], 1)
                wait_apart(pool, t["halves"], rnd + 2)

        @block.vector
        def _(v):
            for k in range(2):
                for carry in (z[k], u[k]):
                    v.memset(carry[:, CHUNK - 1:CHUNK], 0.0)
                v.memset(m[k][:, CHUNK:CHUNK + 1], 0.0)
            v.sem_inc(t["transposed"], 2)
            v.sem_inc(t["round_set"], 1)
            v.drain()
            with v.Fori(0, ROUNDS) as rnd:
                base = v.snap(rnd * EDGE_CHUNKS)

                def spread_1(c, k):
                    g = base + c
                    v.wait_ge(t["rows_in"], g + 3)
                    partial_stats(v, [tile(hs[k], j) for j in tiles] + [ring(g, j) for j in tiles], t["st1"])

                def moments_1(c, k):
                    moments_of(v, t["st1"], ma[k], 2 * TILES).then_inc(t["stats1"], 1)

                def weigh(c, k):
                    g = base + c
                    v.wait_ge(t["rstd1"], g + 1)
                    v.wait_ge(t["transposed"], g + 1)
                    rows = [tile(hs[k], j) for j in tiles] + [ring(g, j) for j in tiles]
                    outs = [tile(xs[k], j) for j in tiles] + [tile(xd[k], j) for j in tiles]
                    for j, (o, h) in enumerate(zip(outs, rows)):
                        v.scalar_tensor_tensor(o, h, ma[k][:, 2 * j:2 * j + 1], w["norm_w"][:, :],
                                               ALU.subtract, ALU.mult)

                def add_bias(c, k):
                    for j, o in enumerate([tile(xs[k], j) for j in tiles] + [tile(xd[k], j) for j in tiles]):
                        v.scalar_tensor_tensor(o, o, ra[k][:, j:j + 1], w["norm_b"][:, :], ALU.mult, ALU.add)

                def spread_2(c, k):
                    partial_stats(v, [tile(xs[k], j) for j in tiles] + [tile(xd[k], j) for j in tiles], t["st2"])

                def moments_2(c, k):
                    moments_of(v, t["st2"], mb[k], 2 * TILES).then_inc(t["stats2"], 1)

                def shift_2(c, k):
                    v.wait_ge(t["rstd2"], base + c + 1)
                    shift_of(v, shift2[k], mb[k], rb[k], 2 * TILES).then_inc(t["shift2"], 1)

                def products(c, k):
                    g = base + c
                    v.wait_ge(t["k_ready"], g + 1)
                    v.wait_ge(t["qv_done"], g + 1)
                    v.scalar_tensor_tensor(att[k][:, :], t["ps_q"][:, :], w["bqkv"][:, 0:1], ks[k][:, :],
                                           ALU.add, ALU.mult)
                    v.tensor_copy(m[k][:, 0:1], m[1 - k][:, CHUNK:CHUNK + 1])

                def running_max(c, k):
                    v.tensor_tensor_scan(m[k][:, 1:1 + CHUNK], w["run_gap"][:, bass.ds(c * CHUNK, CHUNK)], att[k][:, :],
                                         m[1 - k][:, CHUNK:CHUNK + 1], ALU.add, ALU.max)

                def arguments(c, k):
                    v.tensor_tensor(d[k][:, 0:CHUNK], m[k][:, 0:CHUNK], m[k][:, 1:1 + CHUNK], ALU.subtract)
                    v.tensor_tensor(d[k][:, CHUNK:2 * CHUNK], att[k][:, :], m[k][:, 1:1 + CHUNK], ALU.subtract)

                def run_starts(c, k):
                    v.tensor_tensor(d[k][:, 0:CHUNK], d[k][:, 0:CHUNK], w["run_gap"][:, bass.ds(c * CHUNK, CHUNK)],
                                    ALU.add).then_inc(t["arg_ready"], 1)

                def sum_e(c, k):
                    v.wait_ge(t["exp_done"], base + c + 1)
                    decay, e = d[k][:, 0:CHUNK], d[k][:, CHUNK:2 * CHUNK]
                    v.scalar_tensor_tensor(t["ve"][:, :], t["ps_v"][:, :], w["bqkv"][:, 2:3], e, ALU.add, ALU.mult)\
                     .then_inc(t["v_used"], 1)
                    v.tensor_tensor_scan(z[k][:, :], decay, e, z[1 - k][:, CHUNK - 1:CHUNK], ALU.mult, ALU.add)

                def sum_ve(c, k):
                    v.tensor_tensor_scan(u[k][:, :], d[k][:, 0:CHUNK], t["ve"][:, :], u[1 - k][:, CHUNK - 1:CHUNK],
                                         ALU.mult, ALU.add).then_inc(t["zu_ready"], 1)

                def softmax_out(c, k):
                    v.wait_ge(t["rz_ready"], base + c + 1)
                    v.tensor_tensor(r[k][:, :], u[k][:, :], rz[k][:, :], ALU.mult).then_inc(t["r_ready"], 1)

                def spread_3(c, k):
                    v.wait_ge(t["r_rows"], base + c + 1)
                    partial_stats(v, [tile(t["ps_r"], j) for j in tiles], t["st3"])

                def moments_3(c, k):
                    moments_of(v, t["st3"], mc[k], TILES).then_inc(t["stats3"], 1)

                def shift_3(c, k):
                    v.wait_ge(t["rstd3"], base + c + 1)
                    shift_of(v, shift3[k], mc[k], rc[k], TILES).then_inc(t["shift3"], 1)

                def new_rows(c, k):
                    g = base + c
                    v.wait_ge(t["y_done"], g + 1)
                    if later(c, 2):
                        v.wait_ge(scattered[k], (g - k) * (DMA * TILES // 2))
                    v.tensor_tensor(new[k][:, :], t["ps_y"][:, :], ring(g, 0, CHUNK), ALU.add)\
                     .then_inc(t["new_ready"], 1)

                run_slots(v, EDGE_CHUNKS, first, [
                    (7, new_rows), (4, sum_e), (5, shift_3), (1, weigh), (None, v.drain), (4, sum_ve),
                    (1, add_bias), (None, v.drain), (2, shift_2), (1, spread_2), (4, softmax_out),
                    (3, products), (None, v.drain), (1, moments_2), (3, running_max), (None, v.drain),
                    (3, arguments), (0, spread_1), (4, spread_3), (None, v.drain), (3, run_starts),
                    (4, moments_3), (0, moments_1)])
                v.tensor_tensor(w["lc4"][:, :], w["lc4"][:, :], w["c4"][:, :], ALU.add)
                v.tensor_tensor(w["neg_row"][:, :], w["neg_row"][:, :], w["c_row"][:, :], ALU.subtract)
                v.drain().then_inc(t["round_set"], 1)

        @block.scalar
        def _(a):
            eps = w["eps_col"][:, 0:1]
            with a.Fori(0, ROUNDS) as rnd:
                base = a.snap(rnd * EDGE_CHUNKS)

                def gelus(c, k):
                    g4 = (base + c) * HC
                    for j in range(HC):
                        a.wait_ge(t["hid_done"], g4 + (j + 1))
                        a.activation(tile(hid[k], j, CHUNK), hid_bank[j % 2][:, :], ACT.Gelu, bias=w["b1"][:, j:j + 1])\
                         .then_inc(t["gelu_done"], 1)

                def gelu_and_log_exp_tables(c, k):
                    gelus(c, k)
                    a.preload_act_table_set("natural_log_exp_and_others")

                def exps(c, k):
                    a.wait_ge(t["arg_ready"], base + c + 1)
                    a.activation(d[k][:, :], d[k][:, :], ACT.Exp).then_inc(t["exp_done"], 1)

                def scaled_k(c, k):
                    a.wait_ge(t["k_done"], base + c + 1)
                    a.activation(ks[k][:, :], t["ps_k"][:, :], ACT.Identity, bias=w["bk_scaled"][:, 0:1],
                                 scale=QK_SCALE).then_inc(t["k_ready"], 1)

                def rstd(ready, mom, log_var, out, n, done):
                    def body(c, k):
                        a.wait_ge(ready, base + c + 1)
                        inverse_std(a, mom[k], log_var, out[k], n, eps).then_inc(done, 1)
                    return body

                def inverse_z(c, k):
                    a.wait_ge(t["zu_ready"], base + c + 1)
                    a.activation(t["lz"][:, :], z[k][:, :], ACT.Ln)
                    a.drain()
                    a.activation(rz[k][:, :], t["lz"][:, :], ACT.Exp, scale=-1.0).then_inc(t["rz_ready"], 1)

                def n3_to_sbuf(c, k):
                    a.wait_ge(t["n3_cols"], base + c + 1)
                    a.activation(nT[k][:, :], t["ps_r"][:, :], ACT.Copy).then_inc(t["nT_ready"], 1)

                def sd_to_sbuf(c, k):
                    a.wait_ge(t["transposed"], base + c + 3)
                    a.activation(sT[k][:, :], t["ps_s"][:, :], ACT.Copy)
                    a.activation(dT[k][:, :], t["ps_d"][:, :], ACT.Copy).then_inc(t["sd_ready"], 1)

                def norm_2(c, k):
                    a.wait_ge(t["shift2"], base + c + 1)
                    outs = [tile(xs[k], j) for j in tiles] + [tile(xd[k], j) for j in tiles]
                    scale_and_shift(a, outs, outs, rb[k], shift2[k]).then_inc(t["x_ready"], 1)

                def norm_3(c, k):
                    a.wait_ge(t["shift3"], base + c + 1)
                    scale_and_shift(a, [tile(n3[k], j) for j in tiles], [tile(t["ps_r"], j) for j in tiles],
                                    rc[k], shift3[k]).then_inc(t["n3_ready"], 1)

                rstd_1 = rstd(t["stats1"], ma, t["lv1"], ra, 2 * TILES, t["rstd1"])
                rstd_2 = rstd(t["stats2"], mb, t["lv2"], rb, 2 * TILES, t["rstd2"])
                rstd_3 = rstd(t["stats3"], mc, t["lv3"], rc, TILES, t["rstd3"])
                run_slots(a, EDGE_CHUNKS, first, [
                    (5, norm_3), (3, sd_to_sbuf), (2, rstd_2), (4, inverse_z), (3, scaled_k),
                    (5, n3_to_sbuf), (2, norm_2), (5, gelu_and_log_exp_tables), (3, exps), (4, rstd_3),
                    (0, rstd_1)])

        @block.tensor
        def _(pe):
            with pe.Fori(0, ROUNDS) as rnd:
                base = pe.snap(rnd * EDGE_CHUNKS)
                pe.wait_ge(t["round_set"], rnd + 1)

                def up(c, k):
                    pe.wait_ge(t["nT_ready"], base + c + 1)
                    g4 = (base + c) * HC
                    for j in range(HC):
                        if j == 1:
                            pe.wait_ge(t["sd_ready"], chunks_before_up(base, c))
                        if later(c, 1) or j > 1:
                            pe.wait_ge(t["gelu_done"], g4 + (j - 1 if j > 1 else 0))
                        pe.matmul(hid_bank[j % 2][:, :], tile(w["w1"], j), nT[k][:, :], start=True, stop=True)\
                          .then_inc(t["hid_done"], 1)

                def r_to_rows(c, k):
                    g = base + c
                    pe.wait_ge(t["r_ready"], g + 1)
                    if later(c, 1):
                        pe.wait_ge(t["nT_ready"], g)
                    for j in tiles:
                        last = pe.transpose(tile(t["ps_r"], j), tile(r[k], j), w["ident"][:, :])
                    last.then_inc(t["r_rows"], 1)

                def qkv(c, k):
                    g = base + c
                    pe.wait_ge(t["sd_ready"], g + 1)
                    if later(c, 1):
                        pe.wait_ge(t["arg_ready"], g)
                    pe.matmul(t["ps_k"][:, :], tile(w["wqkv"], 1), dT[k][:, :], start=True, stop=True).then_inc(t["k_done"], 1)
                    pe.matmul(t["ps_q"][:, :], tile(w["wqkv"], 0), sT[k][:, :], start=True, stop=True)
                    if later(c, 1):
                        pe.wait_ge(t["v_used"], g)
                    pe.matmul(t["ps_v"][:, :], tile(w["wqkv"], 2), sT[k][:, :], start=True, stop=True).then_inc(t["qv_done"], 1)

                def down(c, k):
                    g = base + c
                    pe.wait_ge(t["gelu_done"], (g + 1) * HC)
                    if later(c, 1):
                        pe.wait_ge(t["new_ready"], g)
                    for j in tiles:
                        pe.matmul(tile(t["ps_y"], j), w["ones_row"][:, :], w["neg_row"][:, :], start=True, stop=False)
                        for i in range(HC):
                            last = pe.matmul(tile(t["ps_y"], j), hid[k][:, i * CHUNK + j * P:i * CHUNK + (j + 1) * P],
                                             tile(w["w2"], i), start=False, stop=i == HC - 1)
                    last.then_inc(t["y_done"], 1)

                def x_to_cols(c, k):
                    g = base + c
                    pe.wait_ge(t["x_ready"], g + 1)
                    if later(c, 1):
                        pe.wait_ge(t["sd_ready"], g)
                    if later(c, 3):
                        pe.wait_ge(t["gelu_done"], (g - 2) * HC)
                    for bank, rows in ((t["ps_s"], xs[k]), (t["ps_d"], xd[k])):
                        for j in tiles:
                            last = pe.transpose(tile(bank, j), tile(rows, j), w["ident"][:, :])
                    last.then_inc(t["transposed"], 1)

                def n3_to_cols(c, k):
                    pe.wait_ge(t["n3_ready"], base + c + 1)
                    for j in tiles:
                        last = pe.transpose(tile(t["ps_r"], j), tile(n3[k], j), w["ident"][:, :])
                    last.then_inc(t["n3_cols"], 1)

                run_slots(pe, EDGE_CHUNKS, first, [
                    (5, down), (4, n3_to_cols), (2, qkv), (3, r_to_rows), (4, up), (1, x_to_cols)])


def close_rounds(nc, w, inp, tables, x1_tab, x2_tab):
    with ExitStack() as ctx:
        t = {"phase": "close"}
        alloc(nc, ctx, t, "x0 x1 h0 h1 a0 a1 b0 b1", [P, UNIT])
        semaphores(nc, ctx, t, "in0 in1 out0 out1 added")
        x, h, a, b = (t["x0"], t["x1"]), (t["h0"], t["h1"]), (t["a0"], t["a1"]), (t["b0"], t["b1"])
        s_in, s_out = (t["in0"], t["in1"]), (t["out0"], t["out1"])
        block = ctx.enter_context(nc.Block())

        @block.sync
        def _(sp):
            def load(c, k):
                sp.dma_start(x[k][:, :], unit(inp["x"], c)).then_inc(s_in[k], DMA)
                sp.dma_start(h[k][:, :], unit(tables, c, NP)).then_inc(s_in[k], DMA)

            def store(c, k):
                wait_apart(sp, t["added"], c + 1)
                sp.dma_start(unit(x1_tab, c), a[k][:, :]).then_inc(s_out[k], DMA)
                sp.dma_start(unit(x2_tab, c), b[k][:, :]).then_inc(s_out[k], DMA)

            run_slots(sp, UNITS, 5, [(2, store), (0, load)])
            for k in range(2):
                sp.wait_ge(s_out[k], 2 * DMA * len(range(k, UNITS, 2)))

        @block.vector
        def _(v):
            def add(c, k):
                v.wait_ge(s_in[k], (c - k) * DMA + 2 * DMA)
                v.tensor_tensor(x[k][:, :], x[k][:, :], h[k][:, :], ALU.add)
                v.drain()
                if later(c, 2):
                    v.wait_ge(s_out[k], (c - k) * DMA)
                for half in range(2):
                    v.tensor_tensor(tile(a[k], half, CHUNK), tile(x[k], half, CHUNK), w["lc4"][:, :], ALU.add)
                v.drain()
                for half in range(2):
                    last = v.tensor_tensor(tile(b[k], half, CHUNK), tile(a[k], half, CHUNK), w["l1_b4"][:, :],
                                           ALU.add)
                last.then_inc(t["added"], 1)

            run_slots(v, UNITS, 5, [(1, add)])


def graph_attention(nc, w, x1_tab, x2_tab, neigh):
    with ExitStack() as ctx:
        t = {"phase": "gat"}
        alloc(nc, ctx, t, "gs0 gs1 gd0 gd1 xs0 xs1 xd0 xd1 sT0 sT1 dT0 dT1 att0 att1 raw "
                          "z0 z1 zc0 zc1 u0 u1 r0 r1 ve lz rz0 rz1 new0 new1", [P, CHUNK])
        alloc(nc, ctx, t, "res_ring", [P, RING * CHUNK])
        alloc(nc, ctx, t, "zeros", [P, UNIT])
        alloc(nc, ctx, t, "m0 m1", [P, 1 + CHUNK])
        alloc(nc, ctx, t, "d0 d1", [P, 2 * CHUNK])
        alloc(nc, ctx, t, "st", [P, 12 * TILES])
        alloc(nc, ctx, t, "mom0 mom1", [P, 4 * TILES])
        alloc(nc, ctx, t, "lv rs0 rs1", [P, 2 * TILES])
        alloc(nc, ctx, t, "idx_read0 idx_read1", [P, 2 * TILES], I32)
        alloc(nc, ctx, t, "idx_end0 idx_end1", [P, TILES], I32)
        alloc(nc, ctx, t, "ps_s ps_d ps_logit ps_v ps_r", [P, CHUNK], F32, "psum")
        semaphores(nc, ctx, t,
                   "idx_made end_made gathered0 gathered1 rows_free stats rstd x_ready transposed sd_ready "
                   "logit_done v_done raw_ready arg_ready exp_done v_used zu_ready rz_ready r_ready r_rows "
                   "new_ready scattered0 scattered1 zeros_made cleared")
        two = lambda name: (t[name + "0"], t[name + "1"])
        gs, gd, xs, xd, sT, dT, att, z, zc, u = (two(n) for n in "gs gd xs xd sT dT att z zc u".split())
        r, rz, new, m, d, mom, rs = (two(n) for n in "r rz new m d mom rs".split())
        idx_read, idx_end, gathered, scattered = (two(n) for n in "idx_read idx_end gathered scattered".split())
        first = 8
        tiles = range(TILES)
        block = ctx.enter_context(nc.Block())

        @block.sync
        def _(sp):
            sp.wait_ge(t["zeros_made"], 1)
            sp.dma_start(unit(neigh, 0), t["zeros"][:, :]).then_inc(t["cleared"], DMA)
            with sp.Fori(1, UNITS) as c:
                sp.wait_ge(t["cleared"], c * DMA)
                sp.dma_start(unit(neigh, c), t["zeros"][:, :]).then_inc(t["cleared"], DMA)
            sp.wait_ge(t["cleared"], UNITS * DMA)

        @block.gpsimd
        def _(pool):
            def gather(c, k):
                pool.wait_ge(t["rows_free"], c + 1)
                cols = bass.ds(c * TILES, TILES)
                pool.tensor_copy(idx_read[k][:, 0:TILES], w["src_idx"][:, cols])
                pool.tensor_copy(idx_read[k][:, TILES:2 * TILES], w["dst_idx"][:, cols]).then_inc(t["idx_made"], 1)
                wait_apart(pool, t["idx_made"], c + 1)
                for rows, at in ((gs[k], 0), (gd[k], TILES)):
                    for j in tiles:
                        pool.indirect_dma_start(
                            out=tile(rows, j), out_offset=None, in_=x1_tab[:, :],
                            in_offset=AX(ap=idx_read[k][:, at + j:at + j + 1], axis=0)).then_inc(gathered[k], DMA)

            def scatter(c, k):
                pool.wait_ge(t["new_ready"], c + 1)
                if later(c, 2):
                    pool.wait_ge(scattered[k], (c - k) * (DMA * TILES // 2))
                pool.tensor_copy(idx_end[k][:, :], w["end_idx"][:, bass.ds(c * TILES, TILES)]).then_inc(t["end_made"], 1)
                wait_apart(pool, t["end_made"], c + 1)
                for j in tiles:
                    pool.indirect_dma_start(
                        out=x2_tab[:, :], out_offset=AX(ap=idx_end[k][:, j:j + 1], axis=0), in_=tile(new[k], j),
                        in_offset=None, bounds_check=NP - 1, oob_is_err=False).then_inc(scattered[k], DMA)

            run_slots(pool, EDGE_CHUNKS, first, [(0, gather), (5, scatter)])
            for k in range(2):
                pool.wait_ge(scattered[k], EDGE_CHUNKS * (DMA * TILES // 2))

        @block.vector
        def _(v):
            v.memset(t["zeros"][:, :], 0.0).then_inc(t["zeros_made"], 1)
            for k in range(2):
                for carry in (z[k], u[k]):
                    v.memset(carry[:, CHUNK - 1:CHUNK], 0.0)
                v.memset(m[k][:, CHUNK:CHUNK + 1], 0.0)
            v.sem_inc(t["rows_free"], 2)
            v.sem_inc(t["transposed"], 2)
            v.drain()

            def ring(c):
                return t["res_ring"][:, bass.ds((c & (RING - 1)) * CHUNK, CHUNK)]

            def stats(c, k):
                v.wait_ge(gathered[k], (c - k) * (DMA * TILES) + 2 * TILES * DMA)
                v.tensor_tensor(ring(c), gd[k][:, :], w["l1_b4"][:, :], ALU.add)
                row_stats(v, [tile(g[k], j) for g in (gs, gd) for j in tiles], t["st"], mom[k]).then_inc(t["stats"], 1)

            def norm(c, k):
                v.wait_ge(t["rstd"], c + 1)
                v.wait_ge(t["transposed"], c + 1)
                normalise(v, [tile(g[k], j) for g in (xs, xd) for j in tiles],
                          [tile(g[k], j) for g in (gs, gd) for j in tiles], mom[k], rs[k]).then_inc(t["x_ready"], 1)
                v.drain().then_inc(t["rows_free"], 1)

            def running_max(c, k):
                v.wait_ge(t["raw_ready"], c + 1)
                v.scalar_tensor_tensor(att[k][:, :], t["raw"][:, :], 0.2, t["raw"][:, :], ALU.mult, ALU.max)
                v.tensor_copy(m[k][:, 0:1], m[1 - k][:, CHUNK:CHUNK + 1])
                v.drain()
                gap = w["run_gap"][:, bass.ds(c * CHUNK, CHUNK)]
                v.tensor_tensor_scan(m[k][:, 1:1 + CHUNK], gap, att[k][:, :],
                                     m[1 - k][:, CHUNK:CHUNK + 1], ALU.add, ALU.max)
                v.drain()
                v.tensor_tensor(d[k][:, 0:CHUNK], m[k][:, 0:CHUNK], m[k][:, 1:1 + CHUNK], ALU.subtract)
                v.tensor_tensor(d[k][:, CHUNK:2 * CHUNK], att[k][:, :], m[k][:, 1:1 + CHUNK], ALU.subtract)
                v.drain()
                v.tensor_tensor(d[k][:, 0:CHUNK], d[k][:, 0:CHUNK], gap, ALU.add).then_inc(t["arg_ready"], 1)

            def run_sums(c, k):
                v.wait_ge(t["exp_done"], c + 1)
                v.wait_ge(t["v_done"], c + 1)
                decay, e = d[k][:, 0:CHUNK], d[k][:, CHUNK:2 * CHUNK]
                v.tensor_tensor(t["ve"][:, :], t["ps_v"][:, :], e, ALU.mult).then_inc(t["v_used"], 1)
                v.tensor_tensor_scan(z[k][:, :], decay, e, z[1 - k][:, CHUNK - 1:CHUNK], ALU.mult, ALU.add)
                v.drain()
                v.tensor_scalar(zc[k][:, :], z[k][:, :], 1e-9, None, ALU.max)
                v.tensor_tensor_scan(u[k][:, :], decay, t["ve"][:, :], u[1 - k][:, CHUNK - 1:CHUNK],
                                     ALU.mult, ALU.add).then_inc(t["zu_ready"], 1)

            def softmax_out(c, k):
                v.wait_ge(t["rz_ready"], c + 1)
                v.tensor_tensor(r[k][:, :], u[k][:, :], rz[k][:, :], ALU.mult).then_inc(t["r_ready"], 1)

            def new_rows(c, k):
                v.wait_ge(t["r_rows"], c + 1)
                if later(c, 2):
                    v.wait_ge(scattered[k], (c - k) * (DMA * TILES // 2))
                v.tensor_tensor(new[k][:, :], t["ps_r"][:, :], ring(c), ALU.add).then_inc(t["new_ready"], 1)

            run_slots(v, EDGE_CHUNKS, first, [(5, softmax_out), (2, norm), (4, run_sums), (3, running_max),
                                              (5, new_rows), (1, stats)])

        @block.scalar
        def _(a):
            def exps(c, k):
                a.wait_ge(t["arg_ready"], c + 1)
                a.activation(d[k][:, :], d[k][:, :], ACT.Exp).then_inc(t["exp_done"], 1)

            def logits(c, k):
                a.wait_ge(t["logit_done"], c + 1)
                a.activation(t["raw"][:, :], t["ps_logit"][:, :], ACT.Copy).then_inc(t["raw_ready"], 1)

            def inverse_z(c, k):
                a.wait_ge(t["zu_ready"], c + 1)
                a.activation(t["lz"][:, :], zc[k][:, :], ACT.Ln)
                a.drain()
                a.activation(rz[k][:, :], t["lz"][:, :], ACT.Exp, scale=-1.0).then_inc(t["rz_ready"], 1)

            def sd_to_sbuf(c, k):
                a.wait_ge(t["transposed"], c + 3)
                a.activation(sT[k][:, :], t["ps_s"][:, :], ACT.Relu)
                a.activation(dT[k][:, :], t["ps_d"][:, :], ACT.Relu).then_inc(t["sd_ready"], 1)

            def rstd(c, k):
                a.wait_ge(t["stats"], c + 1)
                inverse_std(a, mom[k], t["lv"], rs[k], 2 * TILES, w["eps_col"][:, 0:1]).then_inc(t["rstd"], 1)

            run_slots(a, EDGE_CHUNKS, first, [(2, log_exp_tables(a)), (4, exps), (3, logits), (4, inverse_z),
                                              (2, sd_to_sbuf), (1, rstd)])

        @block.tensor
        def _(pe):
            def r_to_rows(c, k):
                pe.wait_ge(t["r_ready"], c + 1)
                if later(c, 1):
                    pe.wait_ge(t["new_ready"], c)
                for j in tiles:
                    last = pe.transpose(tile(t["ps_r"], j), tile(r[k], j), w["ident"][:, :])
                last.then_inc(t["r_rows"], 1)

            def project(c, k):
                pe.wait_ge(t["sd_ready"], c + 1)
                if later(c, 1):
                    pe.wait_ge(t["raw_ready"], c)
                pe.matmul(t["ps_logit"][:, :], w["l1_wsrc"][:, :], sT[k][:, :], start=True, stop=False)
                pe.matmul(t["ps_logit"][:, :], w["l1_wdst"][:, :], dT[k][:, :], start=False, stop=True).then_inc(t["logit_done"], 1)
                if later(c, 1):
                    pe.wait_ge(t["v_used"], c)
                pe.matmul(t["ps_v"][:, :], w["l1_w"][:, :], sT[k][:, :], start=True, stop=True).then_inc(t["v_done"], 1)

            def x_to_cols(c, k):
                pe.wait_ge(t["x_ready"], c + 1)
                if later(c, 1):
                    pe.wait_ge(t["sd_ready"], c)
                for bank, rows in ((t["ps_s"], xs[k]), (t["ps_d"], xd[k])):
                    for j in tiles:
                        last = pe.transpose(tile(bank, j), tile(rows, j), w["ident"][:, :])
                last.then_inc(t["transposed"], 1)

            run_slots(pe, EDGE_CHUNKS, first, [(5, r_to_rows), (3, project), (2, x_to_cols)])


def average_neighbours(nc, w, name, x_tab, weight, neigh):
    with ExitStack() as ctx:
        t = {"phase": name}
        alloc(nc, ctx, t, "gs0 gs1 xs0 xs1 sT0 sT1 same0 same1 sum0 sum1 new0 new1", [P, CHUNK])
        alloc(nc, ctx, t, "st", [P, 6 * TILES])
        alloc(nc, ctx, t, "mom0 mom1", [P, 2 * TILES])
        alloc(nc, ctx, t, "lv rs0 rs1", [P, TILES])
        alloc(nc, ctx, t, "idx_read0 idx_read1 idx_end0 idx_end1", [P, TILES], I32)
        alloc(nc, ctx, t, "ps_s ps_o", [P, CHUNK], F32, "psum")
        semaphores(nc, ctx, t, "idx_made end_made gathered0 gathered1 rows_free stats rstd x_ready "
                               "transposed s_ready sum_ready out_done new_ready scattered0 scattered1")
        two = lambda name: (t[name + "0"], t[name + "1"])
        gs, xs, sT, same, total, new, mom, rs = (two(n) for n in "gs xs sT same sum new mom rs".split())
        idx_read, idx_end, gathered, scattered = (two(n) for n in "idx_read idx_end gathered scattered".split())
        first = 6
        tiles = range(TILES)
        block = ctx.enter_context(nc.Block())

        @block.gpsimd
        def _(pool):
            def gather(c, k):
                pool.wait_ge(t["rows_free"], c + 1)
                pool.tensor_copy(idx_read[k][:, :], w["src_idx"][:, bass.ds(c * TILES, TILES)]).then_inc(t["idx_made"], 1)
                wait_apart(pool, t["idx_made"], c + 1)
                for j in tiles:
                    pool.indirect_dma_start(out=tile(gs[k], j), out_offset=None, in_=x_tab[:, :],
                                            in_offset=AX(ap=idx_read[k][:, j:j + 1], axis=0)).then_inc(gathered[k], DMA)

            def scatter(c, k):
                pool.wait_ge(t["new_ready"], c + 1)
                if later(c, 2):
                    pool.wait_ge(scattered[k], (c - k) * (DMA * TILES // 2))
                pool.tensor_copy(idx_end[k][:, :], w["end_idx"][:, bass.ds(c * TILES, TILES)]).then_inc(t["end_made"], 1)
                wait_apart(pool, t["end_made"], c + 1)
                for j in tiles:
                    pool.indirect_dma_start(
                        out=neigh[:, :], out_offset=AX(ap=idx_end[k][:, j:j + 1], axis=0), in_=tile(new[k], j),
                        in_offset=None, bounds_check=NP - 1, oob_is_err=False).then_inc(scattered[k], DMA)

            run_slots(pool, EDGE_CHUNKS, first, [(0, gather), (4, scatter)])
            for k in range(2):
                pool.wait_ge(scattered[k], EDGE_CHUNKS * (DMA * TILES // 2))

        @block.vector
        def _(v):
            for k in range(2):
                v.memset(total[k][:, CHUNK - 1:CHUNK], 0.0)
            v.sem_inc(t["rows_free"], 2)
            v.sem_inc(t["transposed"], 2)
            v.drain()

            def stats(c, k):
                v.wait_ge(gathered[k], (c - k) * (DMA * TILES // 2) + TILES * DMA)
                row_stats(v, [tile(gs[k], j) for j in tiles], t["st"], mom[k]).then_inc(t["stats"], 1)

            def norm(c, k):
                v.wait_ge(t["rstd"], c + 1)
                v.wait_ge(t["transposed"], c + 1)
                normalise(v, [tile(xs[k], j) for j in tiles], [tile(gs[k], j) for j in tiles],
                          mom[k], rs[k]).then_inc(t["x_ready"], 1)
                v.drain().then_inc(t["rows_free"], 1)

            def run_sum(c, k):
                v.tensor_scalar(same[k][:, :], w["run_gap"][:, bass.ds(c * CHUNK, CHUNK)], -1.0 / GAP, 1.0,
                                ALU.mult, ALU.add)
                v.drain()
                v.wait_ge(t["s_ready"], c + 1)
                v.tensor_tensor_scan(total[k][:, :], same[k][:, :], sT[k][:, :],
                                     total[1 - k][:, CHUNK - 1:CHUNK], ALU.mult, ALU.add).then_inc(t["sum_ready"], 1)
                v.drain()

            def new_rows(c, k):
                v.wait_ge(t["out_done"], c + 1)
                if later(c, 2):
                    v.wait_ge(scattered[k], (c - k) * (DMA * TILES // 2))
                for j in tiles:
                    last = v.tensor_scalar(tile(new[k], j), tile(t["ps_o"], j), w["rdeg"][:, bass.ds(c * TILES + j, 1)],
                                           None, ALU.mult)
                last.then_inc(t["new_ready"], 1)

            run_slots(v, EDGE_CHUNKS, first, [(4, new_rows), (3, run_sum), (2, norm), (1, stats)])

        @block.scalar
        def _(a):
            def to_sbuf(c, k):
                a.wait_ge(t["transposed"], c + 3)
                a.activation(sT[k][:, :], t["ps_s"][:, :], ACT.Relu).then_inc(t["s_ready"], 1)

            def rstd(c, k):
                a.wait_ge(t["stats"], c + 1)
                inverse_std(a, mom[k], t["lv"], rs[k], TILES, w["eps_col"][:, 0:1]).then_inc(t["rstd"], 1)

            run_slots(a, EDGE_CHUNKS, first, [(0, log_exp_tables(a)), (2, to_sbuf), (1, rstd)])

        @block.tensor
        def _(pe):
            def project(c, k):
                pe.wait_ge(t["sum_ready"], c + 1)
                if later(c, 1):
                    pe.wait_ge(t["new_ready"], c)
                for j in tiles:
                    last = pe.matmul(tile(t["ps_o"], j), tile(total[k], j), weight[:, :], start=True, stop=True)
                last.then_inc(t["out_done"], 1)

            def x_to_cols(c, k):
                pe.wait_ge(t["x_ready"], c + 1)
                if later(c, 1):
                    pe.wait_ge(t["s_ready"], c)
                for j in tiles:
                    last = pe.transpose(tile(t["ps_s"], j), tile(xs[k], j), w["ident"][:, :])
                last.then_inc(t["transposed"], 1)

            run_slots(pe, EDGE_CHUNKS, first, [(3, project), (2, x_to_cols)])


def node_layer(nc, w, name, x_tab, neigh, out_tab, deep):
    with ExitStack() as ctx:
        t = {"phase": name}
        alloc(nc, ctx, t, "cn0 cn1 xn0 xn1 hT0 hT1 h10 h11 h20 h21 new0 new1", [P, CHUNK])
        alloc(nc, ctx, t, "x_ring", [P, RING * CHUNK])
        alloc(nc, ctx, t, "st0 st1", [P, 6 * TILES])
        alloc(nc, ctx, t, "mom0 mom1", [P, 2 * TILES])
        alloc(nc, ctx, t, "lv0 lv1 rs0 rs1", [P, TILES])
        alloc(nc, ctx, t, "ps_s ps_o ps_1 ps_2", [P, CHUNK], F32, "psum")
        semaphores(nc, ctx, t, "x_in0 x_in1 n_in0 n_in1 out0 out1 stats rstd x_ready transposed h_ready "
                               "first_done h1_ready second_done h2_ready out_done new_ready")
        two = lambda name: (t[name + "0"], t[name + "1"])
        cn, xn, hT, h1, h2, new, st, mom, lv, rs = (two(n) for n in "cn xn hT h1 h2 new st mom lv rs".split())
        x_in, n_in, s_out = (two(n) for n in "x_in n_in out".split())
        last_lag = 6 if deep else 5
        neigh_lag = 3 if deep else 4
        first = 8
        tiles = range(TILES)
        block = ctx.enter_context(nc.Block())

        def ring(c, j=0, width=D):
            return t["x_ring"][:, bass.ds((c & (RING - 1)) * CHUNK + j * D, width)]

        @block.sync
        def _(sp):
            def earlier_x(c, k):
                if later(c, 2):
                    sp.wait_ge(x_in[k], (c - k) * (DMA // 2))

            def load_x(c, k):
                sp.dma_start(ring(c, 0, CHUNK), nodes(x_tab, c)).then_inc(x_in[k], DMA)

            def neigh_free(c, k):
                if later(c, 2):
                    wait_apart(sp, t["first_done" if deep else "out_done"], c - 1)

            def load_neigh(c, k):
                sp.dma_start(cn[k][:, :], nodes(neigh, c)).then_inc(n_in[k], DMA)

            def store(c, k):
                wait_apart(sp, t["new_ready"], c + 1)
                sp.dma_start(nodes(out_tab, c), new[k][:, :]).then_inc(s_out[k], DMA)

            run_slots(sp, NODE_CHUNKS, first, [(last_lag + 1, store), (neigh_lag, neigh_free), (0, earlier_x),
                                               (neigh_lag, load_neigh), (0, load_x)])
            for k in range(2):
                sp.wait_ge(s_out[k], DMA * (NODE_CHUNKS // 2))

        @block.vector
        def _(v):
            v.sem_inc(t["transposed"], 2)

            def stats(c, k):
                v.wait_ge(x_in[k], (c - k) * (DMA // 2) + DMA)
                row_stats(v, [ring(c, j) for j in tiles], st[k], mom[k]).then_inc(t["stats"], 1)

            def norm(c, k):
                v.wait_ge(t["rstd"], c + 1)
                v.wait_ge(t["transposed"], c + 1)
                normalise(v, [tile(xn[k], j) for j in tiles], [ring(c, j) for j in tiles],
                          mom[k], rs[k]).then_inc(t["x_ready"], 1)

            def new_rows(c, k):
                v.wait_ge(t["out_done"], c + 1)
                if later(c, 2):
                    v.wait_ge(s_out[k], (c - k) * (DMA // 2))
                last = v.tensor_tensor(new[k][:, :], t["ps_o"][:, :], ring(c, 0, CHUNK), ALU.add)
                if deep:
                    v.drain()
                    last = v.tensor_tensor(new[k][:, :], new[k][:, :], w["l3_b4"][:, :], ALU.add)
                last.then_inc(t["new_ready"], 1)

            run_slots(v, NODE_CHUNKS, first, [(2, stats), (3, norm), (last_lag, new_rows)])

        @block.scalar
        def _(a):
            def rstd(c, k):
                a.wait_ge(t["stats"], c + 1)
                inverse_std(a, mom[k], lv[k], rs[k], TILES, w["eps_col"][:, 0:1]).then_inc(t["rstd"], 1)

            def to_sbuf(c, k):
                a.wait_ge(t["transposed"], c + 3)
                a.activation(hT[k][:, :], t["ps_s"][:, :], ACT.Relu).then_inc(t["h_ready"], 1)

            def first_relu(c, k):
                a.wait_ge(t["first_done"], c + 1)
                a.activation(h1[k][:, :], t["ps_1"][:, :], ACT.Relu, bias=w["l3_bself"][:, 0:1]).then_inc(t["h1_ready"], 1)

            def second_relu(c, k):
                a.wait_ge(t["second_done"], c + 1)
                a.activation(h2[k][:, :], t["ps_2"][:, :], ACT.Relu, bias=w["l3_bfc1"][:, 0:1]).then_inc(t["h2_ready"], 1)

            more = [(5, second_relu), (4, first_relu)] if deep else []
            run_slots(a, NODE_CHUNKS, first, [(0, log_exp_tables(a)), (2, rstd)] + more + [(3, to_sbuf)])

        @block.tensor
        def _(pe):
            def x_to_cols(c, k):
                pe.wait_ge(t["x_ready"], c + 1)
                if later(c, 1):
                    pe.wait_ge(t["h_ready"], c)
                for j in tiles:
                    last = pe.transpose(tile(t["ps_s"], j), tile(xn[k], j), w["ident"][:, :])
                last.then_inc(t["transposed"], 1)

            def layer_2(c, k):
                pe.wait_ge(t["h_ready"], c + 1)
                pe.wait_ge(n_in[k], (c - k) * (DMA // 2) + DMA)
                if later(c, 1):
                    pe.wait_ge(t["new_ready"], c)
                pe.matmul(t["ps_o"][:, :], w["ones_row"][:, :], w["l2_b4"][:, :], start=True, stop=False)
                for j in tiles:
                    pe.matmul(tile(t["ps_o"], j), tile(hT[k], j), w["l2_wT"][:, :], start=False, stop=False)
                pe.matmul(t["ps_o"][:, :], w["ident"][:, :], cn[k][:, :], start=False, stop=True).then_inc(t["out_done"], 1)

            def self_and_neigh(c, k):
                pe.wait_ge(t["h_ready"], c + 1)
                pe.wait_ge(n_in[k], (c - k) * (DMA // 2) + DMA)
                if later(c, 1):
                    pe.wait_ge(t["h1_ready"], c)
                pe.matmul(t["ps_1"][:, :], w["l3_self"][:, :], hT[k][:, :], start=True, stop=False)
                for j in tiles:
                    last = pe.matmul(tile(t["ps_1"], j), tile(cn[k], j), w["ident"][:, :], start=False, stop=j == TILES - 1)
                last.then_inc(t["first_done"], 1)

            def fc1(c, k):
                pe.wait_ge(t["h1_ready"], c + 1)
                if later(c, 1):
                    pe.wait_ge(t["h2_ready"], c)
                pe.matmul(t["ps_2"][:, :], w["l3_fc1"][:, :], h1[k][:, :], start=True, stop=True).then_inc(t["second_done"], 1)

            def fc2(c, k):
                pe.wait_ge(t["h2_ready"], c + 1)
                if later(c, 1):
                    pe.wait_ge(t["new_ready"], c)
                for j in tiles:
                    last = pe.matmul(tile(t["ps_o"], j), tile(h2[k], j), w["l3_fc2"][:, :], start=True, stop=True)
                last.then_inc(t["out_done"], 1)

            after = [(6, fc2), (5, fc1), (4, self_and_neigh)] if deep else [(5, layer_2)]
            run_slots(pe, NODE_CHUNKS, first, after + [(3, x_to_cols)])


def bass_four_graph_layers(nc, inp, out):
    with ExitStack() as ctx:
        w = {"phase": "all"}
        alloc(nc, ctx, w, "wqkv", [P, 3 * D])
        alloc(nc, ctx, w, "w1", [P, HIDDEN])
        alloc(nc, ctx, w, "w2", [P, HC * D])
        alloc(nc, ctx, w, "bqkv", [P, 3])
        alloc(nc, ctx, w, "bk_scaled l3_bself l3_bfc1 eps_col", [P, 1])
        alloc(nc, ctx, w, "b1", [P, HC])
        alloc(nc, ctx, w, "norm_w norm_b ident l1_w l1_wsrc l1_wdst l2_wT l3_neigh l3_self l3_fc1 l3_fc2", [P, D])
        alloc(nc, ctx, w, "l3_b4 lc4 c4 l1_b4", [P, CHUNK])
        alloc(nc, ctx, w, "l2_b4", [1, CHUNK])
        alloc(nc, ctx, w, "ones_row neg_row c_row", [1, D])
        alloc(nc, ctx, w, "src_idx dst_idx end_idx", [P, EDGE_CHUNKS * TILES], I32)
        alloc(nc, ctx, w, "rdeg", [P, EDGE_CHUNKS * TILES])
        alloc(nc, ctx, w, "run_gap", [P, EP], BF16)
        dram = lambda name, rows: nc.dram_tensor(name, [rows, D], F32).ap()
        tables, x1_tab, x2_tab, x3_tab, neigh = (dram(n, r) for n, r in (
            ("h_tables", 2 * NP), ("x1_table", NP), ("x2_table", NP), ("x3_table", NP), ("neighbours", NP)))
        setup(nc, w, inp)
        start_tables(nc, w, inp, tables)
        attention_rounds(nc, w, tables)
        close_rounds(nc, w, inp, tables, x1_tab, x2_tab)
        graph_attention(nc, w, x1_tab, x2_tab, neigh)
        average_neighbours(nc, w, "mean2", x2_tab, w["l2_wT"], neigh)
        node_layer(nc, w, "nodes2", x2_tab, neigh, x3_tab, deep=False)
        average_neighbours(nc, w, "mean3", x3_tab, w["l3_neigh"], neigh)
        node_layer(nc, w, "nodes3", x3_tab, neigh, out, deep=True)


_NAMES = ['L0_gnn_norm_w', 'L0_gnn_norm_b', 'L0_gnn_nin_w', 'L0_gnn_nin_b', 'L0_gnn_Wqkv', 'L0_gnn_no_w',
          'L0_gnn_no_b', 'L0_gnn_W1', 'L0_gnn_b1', 'L0_gnn_W2', 'L0_gnn_b2', 'L1_gnn_W', 'L1_gnn_att',
          'L1_gnn_bias', 'L2_gnn_W', 'L2_gnn_b', 'L3_gnn_W_neigh', 'L3_gnn_W_self', 'L3_gnn_b_self',
          'L3_gnn_W_fc1', 'L3_gnn_b_fc1', 'L3_gnn_W_fc2', 'L3_gnn_b_fc2']


def kernel(**inputs):
    import numpy as np
    import concourse.bacc as bacc
    from concourse.bass_utils import run_bass_kernel_spmd

    nc = bacc.Bacc("TRN2", target_bir_lowering=False, num_devices=1)
    arrays = {n: np.ascontiguousarray(inputs[n]) for n in _NAMES}
    x = np.asarray(inputs["x"])
    arrays["x"] = np.concatenate([x, np.zeros((NP - N, D), x.dtype)])
    src, dst = np.asarray(inputs["src"]), np.asarray(inputs["dst"])
    pad = lambda a, fill, n: np.concatenate([a, np.full(n, fill, a.dtype)])
    tiles = lambda a: np.ascontiguousarray(a.reshape(EP // P, P).T)
    ext = pad(dst, N, EP + 1 - E)
    arrays["src_t"] = tiles(pad(src, 0, EP - E))
    arrays["dst_t"] = tiles(ext[:EP])
    arrays["dst_next_t"] = tiles(ext[1:EP + 1])
    arrays["dst_ext"] = np.concatenate([np.full(1, -1, dst.dtype), ext[:EP]])
    inp = {n: nc.dram_tensor(f"in_{n}", a.shape, mybir.dt.from_np(a.dtype), kind="ExternalInput").ap()
           for n, a in arrays.items()}
    out = nc.dram_tensor("out_0", (NP, D), F32, kind="ExternalOutput").ap()
    bass_four_graph_layers(nc, inp, out)
    r = run_bass_kernel_spmd(nc, [{f"in_{n}": a for n, a in arrays.items()}], core_ids=[0])
    return r.results[0]["out_0"][:N]
```
